# Optimizing a Trainium2 kernel written in Bass

```python
import numpy as np
import jax
import jax.numpy as jnp

def _softmax(x, axis=-1):
    return jax.nn.softmax(x, axis=axis)

def _gelu(x):
    return jax.nn.gelu(x, approximate=True)

def _silu(x):
    return jax.nn.silu(x)

def _sigmoid(x):
    return jax.nn.sigmoid(x)

def _layernorm(x, axis=-1, eps=1e-05):
    m = jnp.mean(x, axis=axis, keepdims=True)
    v = jnp.var(x, axis=axis, keepdims=True)
    return (x - m) / jnp.sqrt(v + eps)

def _scatter_add(tgt, idx, src, axis=0):
    return tgt.at[idx].add(src)

def _segment_sum(src, seg, n):
    return jax.ops.segment_sum(src, seg, n)
kernel_name = 'mk_rec_standalone_d1_rec_r8_1b6151'

def setup_inputs(seed: int=0):
    np.random.seed(seed)
    _w = jnp.asarray

    def _rec_inputs():
        import jax
        import jax.numpy as jnp
        _rk = jax.random.key(seed)
        r_user_dense = 0.00708528 + 1.00131 * jax.random.normal(jax.random.fold_in(_rk, 1), (1024, 25), jnp.float32)
        r_user_id = jax.random.randint(jax.random.fold_in(_rk, 2), (1024,), 78, 199964, jnp.int32)
        r_item_id = jax.random.randint(jax.random.fold_in(_rk, 3), (1024,), 202, 499889, jnp.int32)
        r_item_category = jax.random.randint(jax.random.fold_in(_rk, 4), (1024,), 0, 999, jnp.int32)
        r_item_dur_bkt = jax.random.randint(jax.random.fold_in(_rk, 5), (1024,), 0, 20, jnp.int32)
        r_item_dense = -0.0146907 + 0.998195 * jax.random.normal(jax.random.fold_in(_rk, 6), (1024, 3), jnp.float32)
        r_history_seq = jnp.stack([jax.random.randint(jax.random.fold_in(jax.random.fold_in(_rk, 7), 0), (1024,), 1, 499901, jnp.int32), jax.random.randint(jax.random.fold_in(jax.random.fold_in(_rk, 7), 1), (1024,), 25, 499996, jnp.int32), jax.random.randint(jax.random.fold_in(jax.random.fold_in(_rk, 7), 2), (1024,), 107, 499691, jnp.int32), jax.random.randint(jax.random.fold_in(jax.random.fold_in(_rk, 7), 3), (1024,), 79, 499987, jnp.int32), jax.random.randint(jax.random.fold_in(jax.random.fold_in(_rk, 7), 4), (1024,), 147, 499988, jnp.int32), jax.random.randint(jax.random.fold_in(jax.random.fold_in(_rk, 7), 5), (1024,), 162, 499975, jnp.int32), jax.random.randint(jax.random.fold_in(jax.random.fold_in(_rk, 7), 6), (1024,), 12, 499903, jnp.int32), jax.random.randint(jax.random.fold_in(jax.random.fold_in(_rk, 7), 7), (1024,), 24, 62481, jnp.int32), jax.random.randint(jax.random.fold_in(jax.random.fold_in(_rk, 7), 8), (1024,), 202, 499826, jnp.int32), jax.random.randint(jax.random.fold_in(jax.random.fold_in(_rk, 7), 9), (1024,), 292, 499962, jnp.int32), jax.random.randint(jax.random.fold_in(jax.random.fold_in(_rk, 7), 10), (1024,), 86, 499927, jnp.int32), jax.random.randint(jax.random.fold_in(jax.random.fold_in(_rk, 7), 11), (1024,), 169, 499927, jnp.int32), jax.random.randint(jax.random.fold_in(jax.random.fold_in(_rk, 7), 12), (1024,), 200, 499925, jnp.int32), jax.random.randint(jax.random.fold_in(jax.random.fold_in(_rk, 7), 13), (1024,), 25, 499941, jnp.int32), jax.random.randint(jax.random.fold_in(jax.random.fold_in(_rk, 7), 14), (1024,), 6, 499886, jnp.int32), jax.random.randint(jax.random.fold_in(jax.random.fold_in(_rk, 7), 15), (1024,), 60, 499829, jnp.int32), jax.random.randint(jax.random.fold_in(jax.random.fold_in(_rk, 7), 16), (1024,), 101, 499979, jnp.int32), jax.random.randint(jax.random.fold_in(jax.random.fold_in(_rk, 7), 17), (1024,), 46, 499982, jnp.int32), jax.random.randint(jax.random.fold_in(jax.random.fold_in(_rk, 7), 18), (1024,), 88, 499983, jnp.int32), jax.random.randint(jax.random.fold_in(jax.random.fold_in(_rk, 7), 19), (1024,), 83, 499979, jnp.int32), jax.random.randint(jax.random.fold_in(jax.random.fold_in(_rk, 7), 20), (1024,), 60, 499934, jnp.int32), jax.random.randint(jax.random.fold_in(jax.random.fold_in(_rk, 7), 21), (1024,), 26, 62499, jnp.int32), jax.random.randint(jax.random.fold_in(jax.random.fold_in(_rk, 7), 22), (1024,), 216, 499958, jnp.int32), jax.random.randint(jax.random.fold_in(jax.random.fold_in(_rk, 7), 23), (1024,), 408, 499983, jnp.int32), jax.random.randint(jax.random.fold_in(jax.random.fold_in(_rk, 7), 24), (1024,), 7, 499855, jnp.int32), jax.random.randint(jax.random.fold_in(jax.random.fold_in(_rk, 7), 25), (1024,), 105, 499915, jnp.int32), jax.random.randint(jax.random.fold_in(jax.random.fold_in(_rk, 7), 26), (1024,), 239, 499924, jnp.int32), jax.random.randint(jax.random.fold_in(jax.random.fold_in(_rk, 7), 27), (1024,), 114, 499865, jnp.int32), jax.random.randint(jax.random.fold_in(jax.random.fold_in(_rk, 7), 28), (1024,), 252, 499581, jnp.int32), jax.random.randint(jax.random.fold_in(jax.random.fold_in(_rk, 7), 29), (1024,), 178, 499989, jnp.int32), jax.random.randint(jax.random.fold_in(jax.random.fold_in(_rk, 7), 30), (1024,), 246, 499589, jnp.int32), jax.random.randint(jax.random.fold_in(jax.random.fold_in(_rk, 7), 31), (1024,), 33, 62500, jnp.int32), jax.random.randint(jax.random.fold_in(jax.random.fold_in(_rk, 7), 32), (1024,), 154, 499967, jnp.int32), jax.random.randint(jax.random.fold_in(jax.random.fold_in(_rk, 7), 33), (1024,), 467, 499862, jnp.int32), jax.random.randint(jax.random.fold_in(jax.random.fold_in(_rk, 7), 34), (1024,), 135, 62492, jnp.int32), jax.random.randint(jax.random.fold_in(jax.random.fold_in(_rk, 7), 35), (1024,), 3, 62494, jnp.int32), jax.random.randint(jax.random.fold_in(jax.random.fold_in(_rk, 7), 36), (1024,), 57, 499793, jnp.int32), jax.random.randint(jax.random.fold_in(jax.random.fold_in(_rk, 7), 37), (1024,), 72, 62493, jnp.int32), jax.random.randint(jax.random.fold_in(jax.random.fold_in(_rk, 7), 38), (1024,), 88, 499836, jnp.int32), jax.random.randint(jax.random.fold_in(jax.random.fold_in(_rk, 7), 39), (1024,), 18, 499999, jnp.int32), jax.random.randint(jax.random.fold_in(jax.random.fold_in(_rk, 7), 40), (1024,), 300, 499694, jnp.int32), jax.random.randint(jax.random.fold_in(jax.random.fold_in(_rk, 7), 41), (1024,), 14, 499661, jnp.int32), jax.random.randint(jax.random.fold_in(jax.random.fold_in(_rk, 7), 42), (1024,), 31, 499803, jnp.int32), jax.random.randint(jax.random.fold_in(jax.random.fold_in(_rk, 7), 43), (1024,), 465, 62493, jnp.int32), jax.random.randint(jax.random.fold_in(jax.random.fold_in(_rk, 7), 44), (1024,), 48, 499980, jnp.int32), jax.random.randint(jax.random.fold_in(jax.random.fold_in(_rk, 7), 45), (1024,), 408, 499709, jnp.int32), jax.random.randint(jax.random.fold_in(jax.random.fold_in(_rk, 7), 46), (1024,), 130, 499865, jnp.int32), jax.random.randint(jax.random.fold_in(jax.random.fold_in(_rk, 7), 47), (1024,), 99, 62468, jnp.int32), jax.random.randint(jax.random.fold_in(jax.random.fold_in(_rk, 7), 48), (1024,), 119, 499588, jnp.int32), jax.random.randint(jax.random.fold_in(jax.random.fold_in(_rk, 7), 49), (1024,), 634, 499993, jnp.int32), jax.random.randint(jax.random.fold_in(jax.random.fold_in(_rk, 7), 50), (1024,), 363, 499807, jnp.int32), jax.random.randint(jax.random.fold_in(jax.random.fold_in(_rk, 7), 51), (1024,), 45, 499859, jnp.int32), jax.random.randint(jax.random.fold_in(jax.random.fold_in(_rk, 7), 52), (1024,), 95, 499923, jnp.int32), jax.random.randint(jax.random.fold_in(jax.random.fold_in(_rk, 7), 53), (1024,), 160, 499715, jnp.int32), jax.random.randint(jax.random.fold_in(jax.random.fold_in(_rk, 7), 54), (1024,), 295, 499985, jnp.int32), jax.random.randint(jax.random.fold_in(jax.random.fold_in(_rk, 7), 55), (1024,), 544, 499998, jnp.int32), jax.random.randint(jax.random.fold_in(jax.random.fold_in(_rk, 7), 56), (1024,), 351, 499933, jnp.int32), jax.random.randint(jax.random.fold_in(jax.random.fold_in(_rk, 7), 57), (1024,), 128, 62486, jnp.int32), jax.random.randint(jax.random.fold_in(jax.random.fold_in(_rk, 7), 58), (1024,), 155, 499986, jnp.int32), jax.random.randint(jax.random.fold_in(jax.random.fold_in(_rk, 7), 59), (1024,), 433, 499591, jnp.int32), jax.random.randint(jax.random.fold_in(jax.random.fold_in(_rk, 7), 60), (1024,), 260, 499990, jnp.int32), jax.random.randint(jax.random.fold_in(jax.random.fold_in(_rk, 7), 61), (1024,), 23, 499887, jnp.int32), jax.random.randint(jax.random.fold_in(jax.random.fold_in(_rk, 7), 62), (1024,), 113, 499519, jnp.int32), jax.random.randint(jax.random.fold_in(jax.random.fold_in(_rk, 7), 63), (1024,), 162, 499956, jnp.int32), jax.random.randint(jax.random.fold_in(jax.random.fold_in(_rk, 7), 64), (1024,), 20, 499900, jnp.int32), jax.random.randint(jax.random.fold_in(jax.random.fold_in(_rk, 7), 65), (1024,), 171, 499915, jnp.int32), jax.random.randint(jax.random.fold_in(jax.random.fold_in(_rk, 7), 66), (1024,), 44, 62463, jnp.int32), jax.random.randint(jax.random.fold_in(jax.random.fold_in(_rk, 7), 67), (1024,), 33, 499742, jnp.int32), jax.random.randint(jax.random.fold_in(jax.random.fold_in(_rk, 7), 68), (1024,), 147, 499844, jnp.int32), jax.random.randint(jax.random.fold_in(jax.random.fold_in(_rk, 7), 69), (1024,), 14, 62469, jnp.int32), jax.random.randint(jax.random.fold_in(jax.random.fold_in(_rk, 7), 70), (1024,), 30, 499679, jnp.int32), jax.random.randint(jax.random.fold_in(jax.random.fold_in(_rk, 7), 71), (1024,), 108, 499986, jnp.int32), jax.random.randint(jax.random.fold_in(jax.random.fold_in(_rk, 7), 72), (1024,), 31, 499805, jnp.int32), jax.random.randint(jax.random.fold_in(jax.random.fold_in(_rk, 7), 73), (1024,), 188, 499838, jnp.int32), jax.random.randint(jax.random.fold_in(jax.random.fold_in(_rk, 7), 74), (1024,), 200, 499829, jnp.int32), jax.random.randint(jax.random.fold_in(jax.random.fold_in(_rk, 7), 75), (1024,), 86, 499925, jnp.int32), jax.random.randint(jax.random.fold_in(jax.random.fold_in(_rk, 7), 76), (1024,), 30, 62497, jnp.int32), jax.random.randint(jax.random.fold_in(jax.random.fold_in(_rk, 7), 77), (1024,), 5, 499994, jnp.int32), jax.random.randint(jax.random.fold_in(jax.random.fold_in(_rk, 7), 78), (1024,), 157, 62489, jnp.int32), jax.random.randint(jax.random.fold_in(jax.random.fold_in(_rk, 7), 79), (1024,), 308, 499949, jnp.int32), jax.random.randint(jax.random.fold_in(jax.random.fold_in(_rk, 7), 80), (1024,), 224, 499994, jnp.int32), jax.random.randint(jax.random.fold_in(jax.random.fold_in(_rk, 7), 81), (1024,), 129, 499759, jnp.int32), jax.random.randint(jax.random.fold_in(jax.random.fold_in(_rk, 7), 82), (1024,), 139, 499812, jnp.int32), jax.random.randint(jax.random.fold_in(jax.random.fold_in(_rk, 7), 83), (1024,), 43, 499980, jnp.int32), jax.random.randint(jax.random.fold_in(jax.random.fold_in(_rk, 7), 84), (1024,), 368, 499775, jnp.int32), jax.random.randint(jax.random.fold_in(jax.random.fold_in(_rk, 7), 85), (1024,), 89, 499985, jnp.int32), jax.random.randint(jax.random.fold_in(jax.random.fold_in(_rk, 7), 86), (1024,), 64, 499926, jnp.int32), jax.random.randint(jax.random.fold_in(jax.random.fold_in(_rk, 7), 87), (1024,), 135, 62476, jnp.int32), jax.random.randint(jax.random.fold_in(jax.random.fold_in(_rk, 7), 88), (1024,), 57, 499871, jnp.int32), jax.random.randint(jax.random.fold_in(jax.random.fold_in(_rk, 7), 89), (1024,), 97, 62495, jnp.int32), jax.random.randint(jax.random.fold_in(jax.random.fold_in(_rk, 7), 90), (1024,), 393, 499977, jnp.int32), jax.random.randint(jax.random.fold_in(jax.random.fold_in(_rk, 7), 91), (1024,), 0, 499853, jnp.int32), jax.random.randint(jax.random.fold_in(jax.random.fold_in(_rk, 7), 92), (1024,), 4, 499956, jnp.int32), jax.random.randint(jax.random.fold_in(jax.random.fold_in(_rk, 7), 93), (1024,), 88, 499917, jnp.int32), jax.random.randint(jax.random.fold_in(jax.random.fold_in(_rk, 7), 94), (1024,), 102, 62481, jnp.int32), jax.random.randint(jax.random.fold_in(jax.random.fold_in(_rk, 7), 95), (1024,), 27, 500001, jnp.int32), jax.random.randint(jax.random.fold_in(jax.random.fold_in(_rk, 7), 96), (1024,), 61, 499998, jnp.int32), jax.random.randint(jax.random.fold_in(jax.random.fold_in(_rk, 7), 97), (1024,), 173, 499967, jnp.int32), jax.random.randint(jax.random.fold_in(jax.random.fold_in(_rk, 7), 98), (1024,), 113, 499814, jnp.int32), jax.random.randint(jax.random.fold_in(jax.random.fold_in(_rk, 7), 99), (1024,), 77, 499997, jnp.int32), jax.random.randint(jax.random.fold_in(jax.random.fold_in(_rk, 7), 100), (1024,), 4, 499999, jnp.int32), jax.random.randint(jax.random.fold_in(jax.random.fold_in(_rk, 7), 101), (1024,), 18, 499543, jnp.int32), jax.random.randint(jax.random.fold_in(jax.random.fold_in(_rk, 7), 102), (1024,), 57, 499971, jnp.int32), jax.random.randint(jax.random.fold_in(jax.random.fold_in(_rk, 7), 103), (1024,), 574, 499985, jnp.int32), jax.random.randint(jax.random.fold_in(jax.random.fold_in(_rk, 7), 104), (1024,), 78, 499991, jnp.int32), jax.random.randint(jax.random.fold_in(jax.random.fold_in(_rk, 7), 105), (1024,), 21, 499941, jnp.int32), jax.random.randint(jax.random.fold_in(jax.random.fold_in(_rk, 7), 106), (1024,), 121, 499991, jnp.int32), jax.random.randint(jax.random.fold_in(jax.random.fold_in(_rk, 7), 107), (1024,), 13, 499942, jnp.int32), jax.random.randint(jax.random.fold_in(jax.random.fold_in(_rk, 7), 108), (1024,), 39, 499961, jnp.int32), jax.random.randint(jax.random.fold_in(jax.random.fold_in(_rk, 7), 109), (1024,), 220, 62489, jnp.int32), jax.random.randint(jax.random.fold_in(jax.random.fold_in(_rk, 7), 110), (1024,), 401, 499998, jnp.int32), jax.random.randint(jax.random.fold_in(jax.random.fold_in(_rk, 7), 111), (1024,), 119, 499942, jnp.int32), jax.random.randint(jax.random.fold_in(jax.random.fold_in(_rk, 7), 112), (1024,), 24, 499922, jnp.int32), jax.random.randint(jax.random.fold_in(jax.random.fold_in(_rk, 7), 113), (1024,), 238, 499965, jnp.int32), jax.random.randint(jax.random.fold_in(jax.random.fold_in(_rk, 7), 114), (1024,), 240, 499956, jnp.int32), jax.random.randint(jax.random.fold_in(jax.random.fold_in(_rk, 7), 115), (1024,), 112, 499905, jnp.int32), jax.random.randint(jax.random.fold_in(jax.random.fold_in(_rk, 7), 116), (1024,), 11, 499973, jnp.int32), jax.random.randint(jax.random.fold_in(jax.random.fold_in(_rk, 7), 117), (1024,), 55, 499996, jnp.int32), jax.random.randint(jax.random.fold_in(jax.random.fold_in(_rk, 7), 118), (1024,), 60, 499926, jnp.int32), jax.random.randint(jax.random.fold_in(jax.random.fold_in(_rk, 7), 119), (1024,), 499, 499993, jnp.int32), jax.random.randint(jax.random.fold_in(jax.random.fold_in(_rk, 7), 120), (1024,), 316, 499916, jnp.int32), jax.random.randint(jax.random.fold_in(jax.random.fold_in(_rk, 7), 121), (1024,), 139, 62482, jnp.int32), jax.random.randint(jax.random.fold_in(jax.random.fold_in(_rk, 7), 122), (1024,), 39, 499570, jnp.int32), jax.random.randint(jax.random.fold_in(jax.random.fold_in(_rk, 7), 123), (1024,), 23, 499913, jnp.int32), jax.random.randint(jax.random.fold_in(jax.random.fold_in(_rk, 7), 124), (1024,), 120, 499918, jnp.int32), jax.random.randint(jax.random.fold_in(jax.random.fold_in(_rk, 7), 125), (1024,), 65, 499751, jnp.int32), jax.random.randint(jax.random.fold_in(jax.random.fold_in(_rk, 7), 126), (1024,), 166, 499877, jnp.int32), jax.random.randint(jax.random.fold_in(jax.random.fold_in(_rk, 7), 127), (1024,), 42, 62443, jnp.int32), jax.random.randint(jax.random.fold_in(jax.random.fold_in(_rk, 7), 128), (1024,), 72, 499786, jnp.int32), jax.random.randint(jax.random.fold_in(jax.random.fold_in(_rk, 7), 129), (1024,), 240, 499727, jnp.int32), jax.random.randint(jax.random.fold_in(jax.random.fold_in(_rk, 7), 130), (1024,), 37, 499863, jnp.int32), jax.random.randint(jax.random.fold_in(jax.random.fold_in(_rk, 7), 131), (1024,), 45, 499979, jnp.int32), jax.random.randint(jax.random.fold_in(jax.random.fold_in(_rk, 7), 132), (1024,), 77, 499961, jnp.int32), jax.random.randint(jax.random.fold_in(jax.random.fold_in(_rk, 7), 133), (1024,), 45, 62491, jnp.int32), jax.random.randint(jax.random.fold_in(jax.random.fold_in(_rk, 7), 134), (1024,), 180, 499997, jnp.int32), jax.random.randint(jax.random.fold_in(jax.random.fold_in(_rk, 7), 135), (1024,), 44, 499839, jnp.int32), jax.random.randint(jax.random.fold_in(jax.random.fold_in(_rk, 7), 136), (1024,), 204, 499989, jnp.int32), jax.random.randint(jax.random.fold_in(jax.random.fold_in(_rk, 7), 137), (1024,), 123, 499994, jnp.int32), jax.random.randint(jax.random.fold_in(jax.random.fold_in(_rk, 7), 138), (1024,), 116, 499982, jnp.int32), jax.random.randint(jax.random.fold_in(jax.random.fold_in(_rk, 7), 139), (1024,), 4, 499796, jnp.int32), jax.random.randint(jax.random.fold_in(jax.random.fold_in(_rk, 7), 140), (1024,), 18, 499818, jnp.int32), jax.random.randint(jax.random.fold_in(jax.random.fold_in(_rk, 7), 141), (1024,), 49, 499747, jnp.int32), jax.random.randint(jax.random.fold_in(jax.random.fold_in(_rk, 7), 142), (1024,), 78, 62499, jnp.int32), jax.random.randint(jax.random.fold_in(jax.random.fold_in(_rk, 7), 143), (1024,), 9, 499887, jnp.int32), jax.random.randint(jax.random.fold_in(jax.random.fold_in(_rk, 7), 144), (1024,), 10, 499837, jnp.int32), jax.random.randint(jax.random.fold_in(jax.random.fold_in(_rk, 7), 145), (1024,), 44, 499718, jnp.int32), jax.random.randint(jax.random.fold_in(jax.random.fold_in(_rk, 7), 146), (1024,), 46, 499790, jnp.int32), jax.random.randint(jax.random.fold_in(jax.random.fold_in(_rk, 7), 147), (1024,), 102, 499860, jnp.int32), jax.random.randint(jax.random.fold_in(jax.random.fold_in(_rk, 7), 148), (1024,), 56, 499949, jnp.int32), jax.random.randint(jax.random.fold_in(jax.random.fold_in(_rk, 7), 149), (1024,), 102, 499943, jnp.int32), jax.random.randint(jax.random.fold_in(jax.random.fold_in(_rk, 7), 150), (1024,), 173, 499975, jnp.int32), jax.random.randint(jax.random.fold_in(jax.random.fold_in(_rk, 7), 151), (1024,), 58, 499861, jnp.int32), jax.random.randint(jax.random.fold_in(jax.random.fold_in(_rk, 7), 152), (1024,), 404, 499933, jnp.int32), jax.random.randint(jax.random.fold_in(jax.random.fold_in(_rk, 7), 153), (1024,), 372, 499907, jnp.int32), jax.random.randint(jax.random.fold_in(jax.random.fold_in(_rk, 7), 154), (1024,), 112, 499934, jnp.int32), jax.random.randint(jax.random.fold_in(jax.random.fold_in(_rk, 7), 155), (1024,), 190, 499588, jnp.int32), jax.random.randint(jax.random.fold_in(jax.random.fold_in(_rk, 7), 156), (1024,), 122, 499690, jnp.int32), jax.random.randint(jax.random.fold_in(jax.random.fold_in(_rk, 7), 157), (1024,), 195, 499833, jnp.int32), jax.random.randint(jax.random.fold_in(jax.random.fold_in(_rk, 7), 158), (1024,), 36, 499778, jnp.int32), jax.random.randint(jax.random.fold_in(jax.random.fold_in(_rk, 7), 159), (1024,), 183, 499773, jnp.int32), jax.random.randint(jax.random.fold_in(jax.random.fold_in(_rk, 7), 160), (1024,), 137, 499858, jnp.int32), jax.random.randint(jax.random.fold_in(jax.random.fold_in(_rk, 7), 161), (1024,), 350, 499946, jnp.int32), jax.random.randint(jax.random.fold_in(jax.random.fold_in(_rk, 7), 162), (1024,), 50, 499969, jnp.int32), jax.random.randint(jax.random.fold_in(jax.random.fold_in(_rk, 7), 163), (1024,), 130, 62481, jnp.int32), jax.random.randint(jax.random.fold_in(jax.random.fold_in(_rk, 7), 164), (1024,), 35, 62491, jnp.int32), jax.random.randint(jax.random.fold_in(jax.random.fold_in(_rk, 7), 165), (1024,), 178, 499753, jnp.int32), jax.random.randint(jax.random.fold_in(jax.random.fold_in(_rk, 7), 166), (1024,), 42, 499805, jnp.int32), jax.random.randint(jax.random.fold_in(jax.random.fold_in(_rk, 7), 167), (1024,), 72, 499809, jnp.int32), jax.random.randint(jax.random.fold_in(jax.random.fold_in(_rk, 7), 168), (1024,), 24, 499902, jnp.int32), jax.random.randint(jax.random.fold_in(jax.random.fold_in(_rk, 7), 169), (1024,), 49, 499991, jnp.int32), jax.random.randint(jax.random.fold_in(jax.random.fold_in(_rk, 7), 170), (1024,), 10, 62447, jnp.int32), jax.random.randint(jax.random.fold_in(jax.random.fold_in(_rk, 7), 171), (1024,), 55, 499979, jnp.int32), jax.random.randint(jax.random.fold_in(jax.random.fold_in(_rk, 7), 172), (1024,), 272, 499465, jnp.int32), jax.random.randint(jax.random.fold_in(jax.random.fold_in(_rk, 7), 173), (1024,), 84, 499923, jnp.int32), jax.random.randint(jax.random.fold_in(jax.random.fold_in(_rk, 7), 174), (1024,), 20, 499923, jnp.int32), jax.random.randint(jax.random.fold_in(jax.random.fold_in(_rk, 7), 175), (1024,), 15, 62499, jnp.int32), jax.random.randint(jax.random.fold_in(jax.random.fold_in(_rk, 7), 176), (1024,), 446, 499994, jnp.int32), jax.random.randint(jax.random.fold_in(jax.random.fold_in(_rk, 7), 177), (1024,), 261, 499995, jnp.int32), jax.random.randint(jax.random.fold_in(jax.random.fold_in(_rk, 7), 178), (1024,), 50, 499947, jnp.int32), jax.random.randint(jax.random.fold_in(jax.random.fold_in(_rk, 7), 179), (1024,), 315, 499732, jnp.int32), jax.random.randint(jax.random.fold_in(jax.random.fold_in(_rk, 7), 180), (1024,), 85, 499841, jnp.int32), jax.random.randint(jax.random.fold_in(jax.random.fold_in(_rk, 7), 181), (1024,), 78, 499982, jnp.int32), jax.random.randint(jax.random.fold_in(jax.random.fold_in(_rk, 7), 182), (1024,), 33, 499990, jnp.int32), jax.random.randint(jax.random.fold_in(jax.random.fold_in(_rk, 7), 183), (1024,), 127, 499958, jnp.int32), jax.random.randint(jax.random.fold_in(jax.random.fold_in(_rk, 7), 184), (1024,), 377, 499967, jnp.int32), jax.random.randint(jax.random.fold_in(jax.random.fold_in(_rk, 7), 185), (1024,), 81, 499885, jnp.int32), jax.random.randint(jax.random.fold_in(jax.random.fold_in(_rk, 7), 186), (1024,), 52, 499983, jnp.int32), jax.random.randint(jax.random.fold_in(jax.random.fold_in(_rk, 7), 187), (1024,), 17, 499982, jnp.int32), jax.random.randint(jax.random.fold_in(jax.random.fold_in(_rk, 7), 188), (1024,), 90, 499989, jnp.int32), jax.random.randint(jax.random.fold_in(jax.random.fold_in(_rk, 7), 189), (1024,), 172, 499973, jnp.int32), jax.random.randint(jax.random.fold_in(jax.random.fold_in(_rk, 7), 190), (1024,), 4, 499981, jnp.int32), jax.random.randint(jax.random.fold_in(jax.random.fold_in(_rk, 7), 191), (1024,), 137, 499884, jnp.int32), jax.random.randint(jax.random.fold_in(jax.random.fold_in(_rk, 7), 192), (1024,), 235, 499926, jnp.int32), jax.random.randint(jax.random.fold_in(jax.random.fold_in(_rk, 7), 193), (1024,), 81, 499919, jnp.int32), jax.random.randint(jax.random.fold_in(jax.random.fold_in(_rk, 7), 194), (1024,), 375, 62476, jnp.int32), jax.random.randint(jax.random.fold_in(jax.random.fold_in(_rk, 7), 195), (1024,), 76, 499994, jnp.int32), jax.random.randint(jax.random.fold_in(jax.random.fold_in(_rk, 7), 196), (1024,), 114, 499833, jnp.int32), jax.random.randint(jax.random.fold_in(jax.random.fold_in(_rk, 7), 197), (1024,), 611, 499981, jnp.int32), jax.random.randint(jax.random.fold_in(jax.random.fold_in(_rk, 7), 198), (1024,), 464, 499747, jnp.int32), jax.random.randint(jax.random.fold_in(jax.random.fold_in(_rk, 7), 199), (1024,), 31, 499615, jnp.int32)], axis=1)
        return (r_user_dense, r_user_id, r_item_id, r_item_category, r_item_dur_bkt, r_item_dense, r_history_seq)
    r_user_dense, r_user_id, r_item_id, r_item_category, r_item_dur_bkt, r_item_dense, r_history_seq = _rec_inputs()

    def _L0_rec_setup():
        import jax, jax.numpy as jnp
        import numpy as np
        B, L = (512, 200)
        N_USERS, N_ITEMS, N_CATS, N_DUR = (25000, 62500, 1000, 20)
        D = 64

        def _lin(k, din, dout):
            kw, kb = jax.random.split(k)
            s = 1.0 / np.sqrt(din)
            return (jax.random.uniform(kw, (din, dout), minval=-s, maxval=s), jax.random.uniform(kb, (dout,), minval=-s, maxval=s))
        key = jax.random.key(seed)
        ks = jax.random.split(key, 20)
        inp = {'user_id': jax.random.randint(ks[0], (B,), 0, N_USERS), 'item_id': jax.random.randint(ks[1], (B,), 0, N_ITEMS), 'item_category': jax.random.randint(ks[2], (B,), 0, N_CATS), 'item_dur_bkt': jax.random.randint(ks[3], (B,), 0, N_DUR), 'user_dense': jax.random.normal(ks[4], (B, 25), dtype=jnp.float32), 'item_dense': jax.random.normal(ks[5], (B, 3), dtype=jnp.float32), 'history_seq': jax.random.randint(ks[6], (B, L), 0, N_ITEMS + 1), 'user_W': 0.01 * jax.random.normal(ks[7], (N_USERS, 64), dtype=jnp.float32), 'item_W': 0.01 * jax.random.normal(ks[8], (N_ITEMS, D), dtype=jnp.float32), 'cat_W': 0.01 * jax.random.normal(ks[9], (N_CATS, 16), dtype=jnp.float32), 'dur_W': 0.01 * jax.random.normal(ks[10], (N_DUR, 8), dtype=jnp.float32), 'hist_W': 0.01 * jax.random.normal(ks[11], (N_ITEMS + 1, D), dtype=jnp.float32)}
        inp['aW0'], inp['ab0'] = _lin(ks[12], 4 * D, 64)
        inp['aW1'], inp['ab1'] = _lin(ks[13], 64, 32)
        inp['aW2'], inp['ab2'] = _lin(ks[14], 32, 1)
        inp['mW0'], inp['mb0'] = _lin(ks[15], 244, 256)
        inp['mW1'], inp['mb1'] = _lin(ks[16], 256, 128)
        inp['mW2'], inp['mb2'] = _lin(ks[17], 128, 1)
        return inp
    _L0_rec_all = _L0_rec_setup()
    _L0_rec_in = {k: v for k, v in _L0_rec_all.items() if k in ('user_W', 'item_W', 'cat_W', 'dur_W', 'hist_W', 'aW0', 'ab0', 'aW1', 'ab1', 'aW2', 'ab2', 'mW0', 'mb0', 'mW1', 'mb1', 'mW2', 'mb2')}
    del _L0_rec_all
    return {'r_user_dense': r_user_dense, 'r_user_id': r_user_id, 'r_item_id': r_item_id, 'r_item_category': r_item_category, 'r_item_dur_bkt': r_item_dur_bkt, 'r_item_dense': r_item_dense, 'r_history_seq': r_history_seq, 'L0_rec_user_W': _L0_rec_in['user_W'], 'L0_rec_item_W': _L0_rec_in['item_W'], 'L0_rec_cat_W': _L0_rec_in['cat_W'], 'L0_rec_dur_W': _L0_rec_in['dur_W'], 'L0_rec_hist_W': _L0_rec_in['hist_W'], 'L0_rec_aW0': _L0_rec_in['aW0'], 'L0_rec_ab0': _L0_rec_in['ab0'], 'L0_rec_aW1': _L0_rec_in['aW1'], 'L0_rec_ab1': _L0_rec_in['ab1'], 'L0_rec_aW2': _L0_rec_in['aW2'], 'L0_rec_ab2': _L0_rec_in['ab2'], 'L0_rec_mW0': _L0_rec_in['mW0'], 'L0_rec_mb0': _L0_rec_in['mb0'], 'L0_rec_mW1': _L0_rec_in['mW1'], 'L0_rec_mb1': _L0_rec_in['mb1'], 'L0_rec_mW2': _L0_rec_in['mW2'], 'L0_rec_mb2': _L0_rec_in['mb2']}

def reference(r_user_dense, r_user_id, r_item_id, r_item_category, r_item_dur_bkt, r_item_dense, r_history_seq, L0_rec_user_W, L0_rec_item_W, L0_rec_cat_W, L0_rec_dur_W, L0_rec_hist_W, L0_rec_aW0, L0_rec_ab0, L0_rec_aW1, L0_rec_ab1, L0_rec_aW2, L0_rec_ab2, L0_rec_mW0, L0_rec_mb0, L0_rec_mW1, L0_rec_mb1, L0_rec_mW2, L0_rec_mb2):
    import jax
    import jax.numpy as jnp

    def _L0_rec_ref(user_id, item_id, item_category, item_dur_bkt, user_dense, item_dense, history_seq, user_W, item_W, cat_W, dur_W, hist_W, aW0, ab0, aW1, ab1, aW2, ab2, mW0, mb0, mW1, mb1, mW2, mb2):
        import jax, jax.numpy as jnp
        import numpy as np
        B, L = (512, 200)
        N_USERS, N_ITEMS, N_CATS, N_DUR = (25000, 62500, 1000, 20)
        D = 64

        def _lin(k, din, dout):
            kw, kb = jax.random.split(k)
            s = 1.0 / np.sqrt(din)
            return (jax.random.uniform(kw, (din, dout), minval=-s, maxval=s), jax.random.uniform(kb, (dout,), minval=-s, maxval=s))
        u_emb = user_W[user_id]
        i_emb = item_W[item_id]
        c_emb = cat_W[item_category]
        d_emb = dur_W[item_dur_bkt]
        hist = hist_W[history_seq]
        t = i_emb[:, None, :]
        tb = jnp.broadcast_to(t, hist.shape)
        feat = jnp.concatenate([hist, tb, hist * t, hist - t], axis=-1)
        h = jax.nn.relu(feat @ aW0 + ab0)
        h = jax.nn.relu(h @ aW1 + ab1)
        scores = (h @ aW2 + ab2)[..., 0]
        pad_mask = history_seq == 0
        scores = jnp.where(pad_mask, jnp.float32(-1000000000.0), scores)
        w = jax.nn.softmax(scores, axis=-1)
        pooled = jnp.einsum('bl,bld->bd', w, hist)
        x = jnp.concatenate([u_emb, i_emb, c_emb, d_emb, user_dense, item_dense, pooled], axis=-1)
        h = jax.nn.relu(x @ mW0 + mb0)
        h = jax.nn.relu(h @ mW1 + mb1)
        logit = (h @ mW2 + mb2)[..., 0]
        return jax.nn.sigmoid(logit)
    y = _L0_rec_ref(r_user_id, r_item_id, r_item_category, r_item_dur_bkt, r_user_dense, r_item_dense, r_history_seq, L0_rec_user_W, L0_rec_item_W, L0_rec_cat_W, L0_rec_dur_W, L0_rec_hist_W, L0_rec_aW0, L0_rec_ab0, L0_rec_aW1, L0_rec_ab1, L0_rec_aW2, L0_rec_ab2, L0_rec_mW0, L0_rec_mb0, L0_rec_mW1, L0_rec_mb1, L0_rec_mW2, L0_rec_mb2)
    return y

_drawn_inputs = setup_inputs


def setup_inputs(seed=0):
    import zlib

    import numpy as np

    out = dict(_drawn_inputs(seed))
    spreads = {}
    factors = {'r_user_dense': 4.528,
     'r_item_dense': 8.0,
     'L0_rec_user_W': 8.0,
     'L0_rec_item_W': 8.0,
     'L0_rec_cat_W': 26.26,
     'L0_rec_dur_W': 32.789,
     'L0_rec_hist_W': 23.265,
     'L0_rec_aW0': 22.1,
     'L0_rec_ab0': 64.0,
     'L0_rec_aW1': 8.0,
     'L0_rec_ab1': 200.0,
     'L0_rec_aW2': 27.31,
     'L0_rec_mW0': 3.986,
     'L0_rec_mb0': 8.0,
     'L0_rec_mW1': 3.887,
     'L0_rec_mb1': 4.655,
     'L0_rec_mW2': 4.662}
    for name, (base, spread) in spreads.items():
        noise = np.random.default_rng([zlib.crc32(name.encode()), seed]).standard_normal(out[name].shape)
        drawn = base * np.exp(spread * noise) if base else spread * noise
        out[name] = jnp.asarray(drawn.astype(out[name].dtype))
    for name, factor in factors.items():
        out[name] = (out[name] * factor).astype(out[name].dtype)
    return out
```

```python
from contextlib import ExitStack

import concourse.bass as bass
from concourse import mybir

ACT = mybir.ActivationFunctionType
ALU = mybir.AluOpType
AX = mybir.AxisListType
F32 = mybir.dt.float32
I32 = mybir.dt.int32
U32 = mybir.dt.uint32


def build_recommender(
    nc, user_dense, user_id, item_id, item_category, item_dur_bkt, item_dense, history_seq,
    user_W, item_W, cat_W, dur_W, hist_W, aW0, ab0, aW1, ab1, aW2, ab2,
    mW0, mb0, mW1, mb1, mW2, mb2, out,
):
    P = 128
    BATCH, HISTORY = history_seq.shape
    TILES = BATCH // P
    D = hist_W.shape[1]
    LAST = hist_W.shape[0] - 1
    LAST_KEY = float(-LAST)
    A0, A1 = aW0.shape[1], aW1.shape[1]
    UNIT = 8
    SLOTS = 2
    HALF = UNIT // 2
    N = HALF * P
    BLOCK = SLOTS * UNIT
    BLOCKS = -(-HISTORY // BLOCK)
    COLS = BLOCKS * BLOCK
    GATHERED = 16 * UNIT
    C_DIM, DUR_DIM = cat_W.shape[1], dur_W.shape[1]
    UD, ID = user_dense.shape[1], item_dense.shape[1]
    X_CAT = 2 * D
    X_DUR = X_CAT + C_DIM
    X_UD = X_DUR + DUR_DIM
    X_ID = X_UD + UD
    X_POOL = X_ID + ID
    X_DIM = X_POOL + D
    M0, M1 = mW0.shape[1], mW1.shape[1]
    X_HI = X_DIM - P
    MASKED = -1000000000.0

    def per_row(ap):
        if len(ap.shape) == 1:
            return ap.rearrange("(p t) -> p t", t=TILES)
        return ap.rearrange("(p t) n -> p t n", t=TILES)

    ctx = ExitStack()
    with ctx:
        def sb(name, shape, dt=F32):
            return ctx.enter_context(nc.sbuf_tensor(name, shape, dt))

        def bank(name):
            return ctx.enter_context(nc.psum_tensor(name, [P, N], F32))

        def sem(name):
            return ctx.enter_context(nc.semaphore(name))

        def slot_sems(name):
            return [sem(f"{name}_{s}") for s in range(SLOTS)]

        ids = sb("ids", [P, 4, TILES], I32)
        ids_f = sb("ids_f", [P, 4, TILES])
        ids_clamped = sb("ids_clamped", [P, 4, TILES], U32)
        history = sb("history", [P, TILES, HISTORY], I32)
        wrapped = sb("wrapped", [P, TILES, HISTORY])
        keys = sb("keys", [P, TILES + 1, HISTORY])
        unsorted = sb("unsorted", [P, HISTORY])
        top = sb("top", [P, SLOTS, UNIT])
        keys_sorted = sb("keys_sorted", [P, TILES + 1, COLS])
        index_sorted = sb("index_sorted", [P, TILES + 1, COLS], U32)
        index_unit = sb("index_unit", [P, SLOTS, UNIT], U32)
        counts = sb("counts", [P, TILES])
        counts_max = sb("counts_max", [TILES, 1])
        needed = sb("needed", [1, TILES + 2], I32)
        identity = sb("identity", [P, P])
        masked = sb("masked", [P, HISTORY])
        wa = sb("wa", [D, A0])
        wb = sb("wb", [D, A0])
        wd = sb("wd", [D, A0])
        w0 = sb("w0", [2 * D, A0])
        w_item = sb("w_item", [D, 2 * A0])
        b0 = sb("b0", [2 * A0, 1])
        w1 = sb("w1", [2 * A0, 2 * A1])
        b1 = sb("b1", [2 * A1, 1])
        w2 = sb("w2", [2 * A1, 2])
        b2 = sb("b2", [P, 1])
        mw0_lo = sb("mw0_lo", [P, M0])
        mw0_hi = sb("mw0_hi", [X_HI, M0])
        mw1 = sb("mw1", [P, M0 // P, M1])
        mw2 = sb("mw2", [M1, 1])
        mbias0 = sb("mbias0", [P, M0 // P])
        mbias1 = sb("mbias1", [M1, 1])
        mbias2 = sb("mbias2", [P, 1])
        last_row = sb("last_row", [P, D])
        itemT = sb("itemT", [D, TILES * P])
        item_term = sb("item_term", [2 * A0, TILES * P])
        feat = sb("feat", [P, SLOTS, UNIT, 2 * D])
        featT = sb("featT", [2 * D, SLOTS, 2 * N])
        h0 = sb("h0", [2 * A0, SLOTS, N])
        h1 = sb("h1", [2 * A1, SLOTS, N])
        scores = sb("scores", [P, COLS])
        last_score = sb("last_score", [P, TILES])
        hist = sb("hist", [P, 2, COLS, D])
        padding = sb("padding", [P, HISTORY], I32)
        neg_max = sb("neg_max", [P, 1])
        expd = sb("expd", [P, HISTORY])
        exp_sum = sb("exp_sum", [P, 1])
        inv_sum = sb("inv_sum", [P, 1])
        last_exp = sb("last_exp", [P, HISTORY])
        last_exp_sum = sb("last_exp_sum", [P, 1])
        own_exp = sb("own_exp", [P, COLS])
        weighted = sb("weighted", [P, BLOCK, D])
        part = sb("part", [P, D])
        pooled = sb("pooled", [P, D])
        x_slots = sb("x_slots", [P, TILES + 1, X_DIM])
        x = x_slots[:, 1:TILES + 1, :]
        neg_mbias2 = sb("neg_mbias2", [P, 1])
        z = sb("z", [P, TILES])
        spare = hist[:, :, :, :].rearrange("p a c d -> p (a c d)")
        ROWS = TILES * P
        xT_lo = spare[:, 0:ROWS]
        xT_hi = spare[0:X_HI, ROWS:2 * ROWS]
        m0 = [spare[:, (2 + m) * ROWS:(3 + m) * ROWS] for m in range(M0 // P)]
        m1 = spare[:, 4 * ROWS:5 * ROWS]

        p_lo, p_hi = bank("p_lo"), bank("p_hi")
        p_h0 = [bank("p_h0_0"), bank("p_h0_1")]
        p_h1, p_score = bank("p_h1"), bank("p_score")
        p_misc, p_misc2 = bank("p_misc"), bank("p_misc2")

        ids_loaded = sem("ids_loaded")
        history_loaded = sem("history_loaded")
        attention_weights_loaded = sem("attention_weights_loaded")
        mlp_loaded = sem("mlp_loaded")
        weights_cleared = sem("weights_cleared")
        identity_step = sem("identity_step")
        ids_step = sem("ids_step")
        keys_step = sem("keys_step")
        counts_step = sem("counts_step")
        counts_transposed = sem("counts_transposed")
        needed_ready = sem("needed_ready")
        items_landed = sem("items_landed")
        embeddings_landed = sem("embeddings_landed")
        fold_step = sem("fold_step")
        cleared = sem("cleared")
        items_transposed = sem("items_transposed")
        itemT_copied = sem("itemT_copied")
        item_term_summed = sem("item_term_summed")
        item_term_ready = sem("item_term_ready")
        last_feat = sem("last_feat")
        last_transposed = sem("last_transposed")
        last_copied_lo = sem("last_copied_lo")
        last_copied_hi = sem("last_copied_hi")
        last_l0 = sem("last_l0")
        last_added = sem("last_added")
        last_relu0 = sem("last_relu0")
        last_l1 = sem("last_l1")
        last_relu1 = sem("last_relu1")
        last_l2 = sem("last_l2")
        last_scored = sem("last_scored")
        landed = slot_sems("landed")
        index_copied = slot_sems("index_copied")
        pool_passed = sem("pool_passed")
        act_passed = sem("act_passed")
        product_ready = slot_sems("product_ready")
        hist_kept = slot_sems("hist_kept")
        transposed_lo = slot_sems("transposed_lo")
        transposed_hi = slot_sems("transposed_hi")
        copied_lo = slot_sems("copied_lo")
        copied_hi = slot_sems("copied_hi")
        layer0_done = slot_sems("layer0_done")
        item_added = slot_sems("item_added")
        relu0_done = slot_sems("relu0_done")
        layer1_done = slot_sems("layer1_done")
        relu1_done = slot_sems("relu1_done")
        layer2_done = slot_sems("layer2_done")
        scored = slot_sems("scored")
        sort_step = sem("sort_step")
        dve_passed = sem("dve_passed")
        block_sorted = sem("block_sorted")
        pool_step = sem("pool_step")
        tile_step = sem("tile_step")
        max_ready = sem("max_ready")
        exp_ready = sem("exp_ready")
        history_pooled = sem("history_pooled")
        xT_ready = sem("xT_ready")
        xT_copied = sem("xT_copied")
        m0_summed = sem("m0_summed")
        m0_ready = sem("m0_ready")
        m1_summed = sem("m1_summed")
        m1_ready = sem("m1_ready")
        m2_summed = sem("m2_summed")
        sigmoid_step = sem("sigmoid_step")
        exp_z = sem("exp_z")
        out_stored = sem("out_stored")

        block = ctx.enter_context(nc.Block())

        def blocks_of(columns):
            return (columns + (BLOCK - 1)) >> 4

        def item_of(t):
            return x_slots[:, bass.ds(t + 1, 1), D:2 * D]

        def columns_of(eng, t):
            return eng.value_load(needed[0:1, bass.ds(t, 1)], min_val=0, max_val=HISTORY)

        @block.sync
        def _(sp):
            for n, table_ids in enumerate((item_id, user_id, item_category, item_dur_bkt)):
                sp.dma_start(ids[:, n, :], per_row(table_ids)).then_inc(ids_loaded, 16)
            sp.dma_start(history[:, :, :], per_row(history_seq)).then_inc(history_loaded, 16)
            for dst, src in (
                (mw0_lo[:, :], mW0[0:P, :]), (mw0_hi[:, :], mW0[P:X_DIM, :]),
                (mw1[:, :, :], mW1.rearrange("(c p) n -> p c n", p=P)), (mw2[:, :], mW2),
                *((mbias0[:, m:m + 1], mb0[m * P:(m + 1) * P].rearrange("(p a) -> p a", a=1)) for m in range(M0 // P)),
                (mbias1[:, :], mb1.rearrange("(p a) -> p a", a=1)),
                (mbias2[:, :], mb2.rearrange("(p a) -> p a", a=1).broadcast_to([P, 1])),
                (x[:, :, X_UD:X_ID], per_row(user_dense)),
                (x[:, :, X_ID:X_POOL], per_row(item_dense)),
            ):
                sp.dma_start(dst, src).then_inc(mlp_loaded, 16)
            sp.wait_ge(sigmoid_step, 2)
            sp.dma_start(per_row(out), z[:, :]).then_inc(out_stored, 16)
            sp.wait_ge(out_stored, 16)

        MLP_LOADS = 16 * (8 + M0 // P)
        ATTENTION_LOADS = 16 * 14

        @block.gpsimd
        def _(pool):
            for counted in index_copied:
                pool.sem_inc(counted, 1)
            nc.gpsimd.memset(w1[:, :], 0.0).then_inc(weights_cleared, 1)
            nc.gpsimd.memset(w2[:, :], 0.0).then_inc(weights_cleared, 1)
            nc.gpsimd.memset(identity[:, :], 0.0).then_inc(identity_step, 1)
            pool.wait_ge(identity_step, 1)
            nc.gpsimd.affine_select(out=identity[:, :], in_=identity[:, :], compare_op=ALU.not_equal, fill=1.0,
                                    base=0, pattern=[[-1, P]], channel_multiplier=1).then_inc(identity_step, 1)
            pool.wait_ge(ids_step, 3)
            for table, n, at, width, landing in (
                (item_W, 0, D, D, items_landed), (user_W, 1, 0, D, embeddings_landed),
                (cat_W, 2, X_CAT, C_DIM, embeddings_landed), (dur_W, 3, X_DUR, DUR_DIM, embeddings_landed),
            ):
                for t in range(TILES):
                    pool.indirect_dma_start(
                        x[:, t, at:at + width], None, table,
                        bass.IndirectOffsetOnAxis(ap=ids_clamped[:, n, t:t + 1], axis=0),
                    ).then_inc(landing, 16)
                if n == 0:
                    nc.gpsimd.memset(keys_sorted[:, :, :], LAST_KEY).then_inc(cleared, 1)
                    nc.gpsimd.memset(own_exp[:, :], 0.0).then_inc(cleared, 1)
                    nc.gpsimd.memset(masked[:, :], MASKED).then_inc(cleared, 1)
                    nc.gpsimd.memset(pooled[:, :], 0.0).then_inc(cleared, 1)
                    nc.gpsimd.memset(inv_sum[:, :], 0.0).then_inc(cleared, 1)
            pool.wait_ge(needed_ready, 1)
            pool.wait_ge(last_transposed, 2)
            base = pool.alloc_register("pool_blocks")
            pool.reg_mov(base, 1)
            with pool.Fori(0, TILES) as t:
                columns = columns_of(pool, t + 1)
                before = pool.snap(base, min_val=1, max_val=TILES * BLOCKS + 1)
                with pool.Fori(0, BLOCKS) as v:
                    with pool.If(columns > v * BLOCK):
                        pool.wait_ge(block_sorted, before + v + 1)
                        for s in range(SLOTS):
                            pool.wait_ge(hist_kept[s], before + v)
                            pool.wait_ge(transposed_hi[s], before + v)
                            nc.gpsimd.tensor_copy(
                                index_unit[:, s, :], index_sorted[:, bass.ds(t, 1), bass.ds(v * BLOCK + s * UNIT, UNIT)]
                                .rearrange("p a c -> p (a c)"),
                            ).then_inc(index_copied[s], 1)
                            pool.wait_ge(index_copied[s], before + v + 1)
                            pool.sem_inc(pool_passed, 1)
                            for k in range(UNIT):
                                pool.indirect_dma_start(
                                    feat[:, s, k, 0:D], None, hist_W,
                                    bass.IndirectOffsetOnAxis(ap=index_unit[:, s, k:k + 1], axis=0),
                                ).then_inc(landed[s], 16)
                pool.reg_add(base, base, pool.snap(blocks_of(columns)))

        @block.scalar
        def _(act):
            for counted in (*hist_kept, *copied_hi, *relu0_done, *relu1_done):
                act.sem_inc(counted, 1)
            loads = [
                (wa[:, :], aW0[0:D, :]), (wb[:, :], aW0[D:2 * D, :]), (w0[D:2 * D, :], aW0[2 * D:3 * D, :]),
                (wd[:, :], aW0[3 * D:4 * D, :]),
                (b2[:, :], ab2.rearrange("(p a) -> p a", a=1).broadcast_to([P, 1])),
                (last_row[:, :], hist_W[LAST:LAST + 1, :].broadcast_to([P, D])),
            ]
            for h in range(2):
                loads += [(b0[h * A0:(h + 1) * A0, :], ab0.rearrange("(p a) -> p a", a=1)),
                          (b1[h * A1:(h + 1) * A1, :], ab1.rearrange("(p a) -> p a", a=1))]
            for h in range(2):
                loads += [(w1[h * A0:(h + 1) * A0, h * A1:(h + 1) * A1], aW1),
                          (w2[h * A1:(h + 1) * A1, h:h + 1], aW2)]
            assert 16 * len(loads) == ATTENTION_LOADS
            for n, (dst, src) in enumerate(loads):
                if n == len(loads) - 4:
                    act.wait_ge(weights_cleared, 2)
                act.dma_start(dst, src).then_inc(attention_weights_loaded, 16)
            act.wait_ge(attention_weights_loaded, ATTENTION_LOADS)

            act.wait_ge(items_transposed, 2)
            nc.scalar.activation(itemT[:, N:2 * N], p_hi[0:D, :], ACT.Copy).then_inc(itemT_copied, 1)
            for c in range(2):
                act.wait_ge(item_term_summed, c + 1)
                nc.scalar.activation(item_term[:, c * N:(c + 1) * N], p_h0[c][:, :], ACT.Identity,
                                     bias=b0[:, :]).then_inc(item_term_ready, 1)
            act.wait_ge(last_transposed, 2)
            nc.scalar.activation(featT[:, 1, N:2 * N], p_hi[:, :], ACT.Copy).then_inc(last_copied_hi, 1)
            act.wait_ge(last_added, 2)
            nc.scalar.activation(h0[:, 1, :], h0[:, 1, :], ACT.Relu).then_inc(last_relu0, 1)
            act.wait_ge(last_l1, 1)
            nc.scalar.activation(h1[:, 1, :], p_h1[0:2 * A1, :], ACT.Relu, bias=b1[:, :]).then_inc(last_relu1, 1)

            act.wait_ge(needed_ready, 1)
            base = act.alloc_register("act_blocks")
            act.reg_mov(base, 1)
            with act.Fori(0, TILES) as t:
                columns = columns_of(act, t + 1)
                before = act.snap(base, min_val=1, max_val=TILES * BLOCKS + 1)
                act.wait_ge(history_pooled, t + 1)
                act.sem_inc(act_passed, 1)
                with act.Fori(0, BLOCKS) as v:
                    with act.If(columns > v * BLOCK):
                        for s in range(SLOTS):
                            act.wait_ge(landed[s], (before + v) * GATHERED)
                            nc.scalar.activation(
                                hist[:, bass.ds(t & 1, 1), bass.ds(v * BLOCK + s * UNIT, UNIT), :]
                                .rearrange("p a c d -> p (a c) d"),
                                feat[:, s, :, 0:D], ACT.Copy).then_inc(hist_kept[s], 1)
                            act.wait_ge(transposed_hi[s], before + v + 1)
                            nc.scalar.activation(featT[:, s, N:2 * N], p_hi[:, :], ACT.Copy).then_inc(copied_hi[s], 1)
                            act.wait_ge(item_added[s], before + v + 1)
                            nc.scalar.activation(h0[:, s, :], h0[:, s, :], ACT.Relu).then_inc(relu0_done[s], 1)
                            act.wait_ge(layer1_done[s], before + v + 1)
                            nc.scalar.activation(h1[:, s, :], p_h1[0:2 * A1, :], ACT.Relu,
                                                 bias=b1[:, :]).then_inc(relu1_done[s], 1)
                act.wait_ge(max_ready, t + 1)
                nc.scalar.activation(expd[:, :], scores[:, 0:HISTORY], ACT.Exp, bias=neg_max[:, :],
                                     accum_out=exp_sum[:, :]).then_inc(exp_ready, 1)
                act.reg_add(base, base, act.snap(blocks_of(columns)))

            act.wait_ge(mlp_loaded, MLP_LOADS)
            for c in range(2):
                act.wait_ge(xT_ready, 2 * c + 2)
                nc.scalar.activation(xT_hi[:, c * N:(c + 1) * N], p_hi[0:X_HI, :], ACT.Copy).then_inc(xT_copied, 1)
            for c in range(2):
                for m in range(M0 // P):
                    act.wait_ge(m0_summed, 2 * c + m + 1)
                    nc.scalar.activation(m0[m][:, c * N:(c + 1) * N], p_h0[m][:, :], ACT.Relu,
                                         bias=mbias0[:, m:m + 1]).then_inc(m0_ready, 1)
                act.wait_ge(m1_summed, c + 1)
                nc.scalar.activation(m1[:, c * N:(c + 1) * N], p_h1[:, :], ACT.Relu,
                                     bias=mbias1[:, :]).then_inc(m1_ready, 1)
            act.wait_ge(m2_summed, 1)
            act.wait_ge(sigmoid_step, 0 + 1)
            nc.scalar.activation(z[:, :], p_misc[:, 0:TILES], ACT.Exp, scale=-1.0,
                                 bias=neg_mbias2[:, :]).then_inc(exp_z, 1)

        @block.tensor
        def _(pe):
            for counted in (*transposed_lo, *transposed_hi, *layer0_done, *layer1_done, *layer2_done):
                pe.sem_inc(counted, 1)
            pe.wait_ge(identity_step, 2)
            pe.wait_ge(counts_step, 1)
            nc.tensor.transpose(p_misc[0:TILES, 0:P], counts[:, :], identity[:, :]).then_inc(counts_transposed, 1)
            pe.wait_ge(counts_step, 2)
            nc.tensor.matmul(p_misc2[0:1, 0:TILES], counts_max[:, :], identity[0:TILES, 0:TILES],
                             start=True, stop=True).then_inc(counts_transposed, 1)
            pe.wait_ge(items_landed, 16 * TILES)
            for c, dst in enumerate((p_lo, p_hi)):
                for k in range(HALF):
                    last = nc.tensor.transpose(dst[0:D, k * P:(k + 1) * P], x[:, c * HALF + k, D:2 * D], identity[:, :])
                last.then_inc(items_transposed, 1)
            pe.wait_ge(fold_step, 3)
            pe.wait_ge(itemT_copied, 2)
            for c in range(2):
                nc.tensor.matmul(p_h0[c][:, :], w_item[:, :], itemT[:, c * N:(c + 1) * N],
                                 start=True, stop=True).then_inc(item_term_summed, 1)
            pe.wait_ge(last_feat, 2)
            for c, dst in enumerate((p_lo, p_hi)):
                for k in range(HALF):
                    last = nc.tensor.transpose(dst[:, k * P:(k + 1) * P], feat[:, 1, c * HALF + k, :], identity[:, :])
                last.then_inc(last_transposed, 1)
            pe.wait_ge(last_copied_lo, 1)
            pe.wait_ge(item_term_ready, 2)
            nc.tensor.matmul(p_h0[1][0:A0, :], w0[:, :], featT[:, 1, 0:N], start=True, stop=True)
            pe.wait_ge(last_copied_hi, 1)
            nc.tensor.matmul(p_h0[1][A0:2 * A0, :], w0[:, :], featT[:, 1, N:2 * N],
                             start=True, stop=True).then_inc(last_l0, 1)
            pe.wait_ge(last_relu0, 1)
            nc.tensor.matmul(p_h1[0:2 * A1, :], w1[:, :], h0[:, 1, :], start=True, stop=True).then_inc(last_l1, 1)
            pe.wait_ge(last_relu1, 1)
            for k in range(HALF):
                last = nc.tensor.matmul(p_score[:, k:UNIT:HALF], h1[:, 1, k * P:(k + 1) * P], w2[:, :],
                                        start=True, stop=True)
            last.then_inc(last_l2, 1)
            pe.wait_ge(last_scored, 1)

            pe.wait_ge(needed_ready, 1)
            base = pe.alloc_register("pe_blocks")
            pe.reg_mov(base, 1)
            with pe.Fori(0, TILES) as t:
                columns = columns_of(pe, t + 1)
                before = pe.snap(base, min_val=1, max_val=TILES * BLOCKS + 1)
                with pe.Fori(0, BLOCKS) as v:
                    with pe.If(columns > v * BLOCK):
                        for s in range(SLOTS):
                            done, this = before + v, before + v + 1
                            previous = done if s == 0 else this
                            pe.wait_ge(product_ready[s], this)
                            pe.wait_ge(copied_lo[1 - s], previous)
                            for k in range(HALF):
                                last = nc.tensor.transpose(p_lo[:, k * P:(k + 1) * P], feat[:, s, k, :], identity[:, :])
                            last.then_inc(transposed_lo[s], 1)
                            pe.wait_ge(copied_hi[1 - s], previous)
                            for k in range(HALF):
                                last = nc.tensor.transpose(p_hi[:, k * P:(k + 1) * P], feat[:, s, HALF + k, :],
                                                           identity[:, :])
                            last.then_inc(transposed_hi[s], 1)
                            pe.wait_ge(item_added[s], done)
                            pe.wait_ge(copied_lo[s], this)
                            nc.tensor.matmul(p_h0[s][0:A0, :], w0[:, :], featT[:, s, 0:N], start=True, stop=True)
                            pe.wait_ge(copied_hi[s], this)
                            nc.tensor.matmul(p_h0[s][A0:2 * A0, :], w0[:, :], featT[:, s, N:2 * N],
                                             start=True, stop=True).then_inc(layer0_done[s], 1)
                            pe.wait_ge(relu1_done[1 - s], previous)
                            pe.wait_ge(relu0_done[s], this)
                            nc.tensor.matmul(p_h1[0:2 * A1, :], w1[:, :], h0[:, s, :],
                                             start=True, stop=True).then_inc(layer1_done[s], 1)
                            pe.wait_ge(scored[s], done)
                            pe.wait_ge(relu1_done[s], this)
                            for k in range(HALF):
                                last = nc.tensor.matmul(p_score[:, s * UNIT + k:(s + 1) * UNIT:HALF],
                                                        h1[:, s, k * P:(k + 1) * P], w2[:, :], start=True, stop=True)
                            last.then_inc(layer2_done[s], 1)
                pe.reg_add(base, base, pe.snap(blocks_of(columns)))

            pe.wait_ge(mlp_loaded, MLP_LOADS)
            pe.wait_ge(embeddings_landed, 3 * 16 * TILES)
            pe.wait_ge(history_pooled, TILES + 2)
            for c in range(2):
                if c:
                    pe.wait_ge(xT_copied, 2 * c)
                for k in range(HALF):
                    last = nc.tensor.transpose(p_lo[:, k * P:(k + 1) * P], x[:, c * HALF + k, 0:P], identity[:, :])
                last.then_inc(xT_ready, 1)
                for k in range(HALF):
                    last = nc.tensor.transpose(p_hi[0:X_HI, k * P:(k + 1) * P], x[:, c * HALF + k, P:X_DIM],
                                               identity[:, :])
                last.then_inc(xT_ready, 1)
            for c in range(2):
                rows = slice(c * N, (c + 1) * N)
                if c == 0:
                    pe.wait_ge(xT_copied, 4)
                for m in range(M0 // P):
                    if c:
                        pe.wait_ge(m0_ready, m + 1)
                    nc.tensor.matmul(p_h0[m][:, :], mw0_lo[:, m * P:(m + 1) * P], xT_lo[:, rows], start=True, stop=False)
                    nc.tensor.matmul(p_h0[m][:, :], mw0_hi[:, m * P:(m + 1) * P], xT_hi[:, rows],
                                     start=False, stop=True).then_inc(m0_summed, 1)
                if c:
                    pe.wait_ge(m1_ready, c)
                for m in range(M0 // P):
                    pe.wait_ge(m0_ready, 2 * c + m + 1)
                    last = nc.tensor.matmul(p_h1[:, :], mw1[:, m, :], m0[m][:, rows], start=(m == 0),
                                            stop=(m == M0 // P - 1))
                last.then_inc(m1_summed, 1)
            pe.wait_ge(m1_ready, 2)
            for t in range(TILES):
                last = nc.tensor.matmul(p_misc[:, t:t + 1], m1[:, t * P:(t + 1) * P], mw2[:, :], start=True, stop=True)
            last.then_inc(m2_summed, 1)

        @block.vector
        def _(dve):
            for counted in (*product_ready, *copied_lo, *item_added, *scored, block_sorted, history_pooled):
                dve.sem_inc(counted, 1)
            dve.sem_inc(sort_step, 4)
            dve.sem_inc(pool_step, 3)
            dve.wait_ge(ids_loaded, 16 * 4)
            tables = (item_W, user_W, cat_W, dur_W)
            for n, table in enumerate(tables):
                last = nc.vector.tensor_scalar(ids_f[:, n, :], ids[:, n, :], 0.0, float(table.shape[0]), ALU.is_lt, ALU.mult)
            last.then_inc(ids_step, 1)
            dve.wait_ge(ids_step, 1)
            nc.vector.tensor_tensor(ids_f[:, :, :], ids_f[:, :, :], ids[:, :, :], ALU.add).then_inc(ids_step, 1)
            dve.wait_ge(ids_step, 2)
            for n, table in enumerate(tables):
                last = nc.vector.tensor_scalar(ids_clamped[:, n, :], ids_f[:, n, :], 0.0, float(table.shape[0] - 1),
                                               ALU.max, ALU.min)
            last.then_inc(ids_step, 1)
            nc.vector.memset(keys[:, TILES, :], LAST_KEY).then_inc(keys_step, 1)
            nc.vector.memset(needed[:, :], 0).then_inc(keys_step, 1)
            dve.wait_ge(history_loaded, 16)
            nc.vector.tensor_scalar(wrapped[:, :, :], history[:, :, :], 0.0, float(LAST + 1), ALU.is_lt,
                                    ALU.mult).then_inc(keys_step, 1)
            dve.wait_ge(keys_step, 3)
            nc.vector.tensor_tensor(wrapped[:, :, :], wrapped[:, :, :], history[:, :, :], ALU.add).then_inc(keys_step, 1)
            dve.wait_ge(keys_step, 4)
            nc.vector.tensor_scalar(wrapped[:, :, :], wrapped[:, :, :], 0.0, float(LAST), ALU.max,
                                    ALU.min).then_inc(keys_step, 1)
            dve.wait_ge(keys_step, 5)
            nc.vector.scalar_tensor_tensor(out=keys[:, 0:TILES, :], in0=history[:, :, :], scalar=0.0,
                                           in1=wrapped[:, :, :], op0=ALU.is_equal, op1=ALU.subtract).then_inc(keys_step, 1)
            dve.wait_ge(keys_step, 6)
            for t in range(TILES):
                last = nc.vector.tensor_scalar(wrapped[:, t, :], keys[:, t, :], LAST_KEY, 0.0, ALU.is_gt, ALU.add,
                                               accum_out=counts[:, t:t + 1])
            last.then_inc(counts_step, 1)
            dve.wait_ge(counts_transposed, 1)
            nc.vector.reduce_max(counts_max[:, :], p_misc[0:TILES, 0:P], AX.X).then_inc(counts_step, 1)
            dve.wait_ge(counts_transposed, 2)
            nc.vector.tensor_copy(needed[:, 1:TILES + 1], p_misc2[0:1, 0:TILES]).then_inc(needed_ready, 1)
            dve.wait_ge(needed_ready, 1)

            def load_keys(t):
                return nc.vector.tensor_copy(unsorted[:, :].unsqueeze(1), keys[:, bass.ds(t, 1), :])

            def sort_block(t, v, sorted_before):
                dve.wait_ge(block_sorted, sorted_before)
                for s in range(SLOTS):
                    dve.wait_ge(sort_step, sorted_before * 4 + 2 * s)
                    dve.sem_inc(dve_passed, 1)
                    nc.vector.max(out=top[:, s, :], in_=unsorted[:, :]).then_inc(sort_step, 1)
                    dve.wait_ge(sort_step, sorted_before * 4 + 2 * s + 1)
                    dve.sem_inc(dve_passed, 1)
                    nc.vector.match_replace(out=unsorted[:, :], in_to_replace=top[:, s, :], in_values=unsorted[:, :],
                                            imm_value=LAST_KEY).then_inc(sort_step, 1)
                columns = bass.ds(v * BLOCK, BLOCK)
                found = top[:, :, :].rearrange("p s c -> p (s c)").unsqueeze(1)
                nc.vector.tensor_copy(keys_sorted[:, bass.ds(t, 1), columns], found)
                nc.vector.tensor_scalar(index_sorted[:, bass.ds(t, 1), columns], found, -1.0, 0.0, ALU.mult,
                                        ALU.max).then_inc(block_sorted, 1)

            def pool_block(t, v, pooled_before):
                columns = bass.ds(v * BLOCK, BLOCK)
                for s in range(SLOTS):
                    dve.wait_ge(hist_kept[s], pooled_before + 1)
                nc.vector.tensor_tensor(
                    weighted[:, :, :], hist[:, bass.ds(t & 1, 1), columns, :].rearrange("p a c d -> p (a c) d"),
                    own_exp[:, columns].unsqueeze(2).broadcast_to([P, BLOCK, D]), ALU.mult).then_inc(pool_step, 1)
                dve.wait_ge(pool_step, pooled_before * 3 + 1)
                nc.vector.tensor_reduce(part[:, :], weighted[:, :, :].rearrange("p c d -> p d c"), op=ALU.add,
                                        axis=AX.X).then_inc(pool_step, 1)
                dve.wait_ge(pool_step, pooled_before * 3 + 2)
                nc.vector.tensor_tensor(pooled[:, :], pooled[:, :], part[:, :], ALU.add).then_inc(pool_step, 1)
                dve.wait_ge(pool_step, pooled_before * 3 + 3)
                dve.sem_inc(dve_passed, 1)

            columns0 = columns_of(dve, 1)
            dve.wait_ge(cleared, 5)
            load_keys(0).then_inc(keys_step, 1)
            dve.wait_ge(keys_step, 7)
            with dve.Fori(0, BLOCKS) as v:
                with dve.If(columns0 > v * BLOCK):
                    sort_block(0, v, v + 1)

            dve.wait_ge(attention_weights_loaded, ATTENTION_LOADS)
            nc.vector.tensor_tensor(w0[0:D, :], wa[:, :], wd[:, :], ALU.add).then_inc(fold_step, 1)
            for h in range(2):
                nc.vector.tensor_tensor(w_item[:, h * A0:(h + 1) * A0], wb[:, :], wd[:, :],
                                        ALU.subtract).then_inc(fold_step, 1)
            dve.wait_ge(items_transposed, 1)
            nc.vector.tensor_copy(itemT[:, 0:N], p_lo[0:D, :]).then_inc(itemT_copied, 1)
            last_rows = last_row[:, :].unsqueeze(1).broadcast_to([P, TILES, D])
            nc.vector.tensor_copy(feat[:, 1, :, 0:D], last_rows).then_inc(last_feat, 1)
            dve.wait_ge(items_landed, 16 * TILES)
            nc.vector.tensor_tensor(feat[:, 1, :, D:2 * D], last_rows, x[:, :, D:2 * D], ALU.mult).then_inc(last_feat, 1)
            dve.wait_ge(last_transposed, 1)
            nc.vector.tensor_copy(featT[:, 1, 0:N], p_lo[:, :]).then_inc(last_copied_lo, 1)
            dve.wait_ge(last_l0, 1)
            for h in range(2):
                part_rows = slice(h * A0, (h + 1) * A0)
                nc.vector.tensor_tensor(h0[part_rows, 1, :], p_h0[1][part_rows, :], item_term[part_rows, h * N:(h + 1) * N],
                                        ALU.add).then_inc(last_added, 1)
            dve.wait_ge(last_l2, 1)
            nc.vector.tensor_scalar(last_score[:, :], p_score[:, 0:TILES], b2[:, :], None, ALU.add).then_inc(last_scored, 1)
            dve.wait_ge(last_scored, 1)

            base = dve.alloc_register("dve_blocks")
            dve.reg_mov(base, 1)
            pooled_base = dve.alloc_register("dve_blocks_pooled")
            dve.reg_mov(pooled_base, 1)
            TILE_STEPS = 8
            with dve.Fori(0, TILES) as t:
                columns_before = columns_of(dve, t)
                columns = columns_of(dve, t + 1)
                columns_next = columns_of(dve, t + 2)
                before = dve.snap(base, min_val=1, max_val=TILES * BLOCKS + 1)
                sorted_before = dve.snap(before + blocks_of(columns))
                pooled_before = dve.snap(pooled_base, min_val=1, max_val=TILES * BLOCKS + 1)
                tile_before = t * TILE_STEPS
                dve.wait_ge(sort_step, sorted_before * 4)
                load_keys(t + 1).then_inc(tile_step, 1)
                nc.vector.tensor_copy(scores[:, :], last_score[:, bass.ds(t, 1)].broadcast_to([P, COLS])).then_inc(tile_step, 1)
                dve.wait_ge(tile_step, tile_before + 2)
                dve.sem_inc(dve_passed, 1)
                with dve.Fori(0, BLOCKS) as v:
                    with dve.If(columns > v * BLOCK):
                        for s in range(SLOTS):
                            this = before + v + 1
                            dve.wait_ge(landed[s], (this - 1) * GATHERED)
                            nc.vector.tensor_tensor(feat[:, s, :, D:2 * D], feat[:, s, :, 0:D],
                                                    item_of(t).broadcast_to([P, UNIT, D]),
                                                    ALU.mult).then_inc(product_ready[s], 1)
                            dve.wait_ge(transposed_lo[s], this)
                            nc.vector.tensor_copy(featT[:, s, 0:N], p_lo[:, :]).then_inc(copied_lo[s], 1)
                            dve.wait_ge(layer0_done[s], this)
                            nc.vector.tensor_tensor(
                                h0[:, s, :].rearrange("p (k b) -> p k b", k=HALF),
                                p_h0[s][:, :].rearrange("p (k b) -> p k b", k=HALF),
                                item_term[:, bass.ds(t * P, P)].unsqueeze(1).broadcast_to([P, HALF, P]),
                                ALU.add).then_inc(item_added[s], 1)
                            dve.wait_ge(layer2_done[s], this)
                            nc.vector.tensor_scalar(scores[:, bass.ds(v * BLOCK + s * UNIT, UNIT)],
                                                    p_score[:, s * UNIT:(s + 1) * UNIT], b2[:, :], None,
                                                    ALU.add).then_inc(scored[s], 1)
                    with dve.If(columns_next > v * BLOCK):
                        sort_block(t + 1, v, sorted_before + v)
                    with dve.If(columns_before > v * BLOCK):
                        pool_block(t + 1, v, pooled_before + v)

                nc.vector.tensor_scalar(x_slots[:, bass.ds(t, 1), X_POOL:X_DIM], pooled[:, :].unsqueeze(1),
                                        inv_sum[:, :], None, ALU.mult).then_inc(history_pooled, 1)
                dve.wait_ge(history_pooled, t + 2)
                tile_keys = keys_sorted[:, bass.ds(t, 1), 0:HISTORY]
                dve.wait_ge(scored[1], before + blocks_of(columns))
                dve.wait_ge(block_sorted, before + blocks_of(columns))
                nc.vector.tensor_scalar(padding[:, :].unsqueeze(1), tile_keys, 0.5, None, ALU.is_gt).then_inc(tile_step, 1)
                dve.wait_ge(tile_step, tile_before + 3)
                dve.sem_inc(dve_passed, 1)
                nc.vector.copy_predicated(scores[:, 0:HISTORY], padding[:, :], masked[:, :]).then_inc(tile_step, 1)
                dve.wait_ge(tile_step, tile_before + 4)
                nc.vector.tensor_reduce(neg_max[:, :], scores[:, 0:HISTORY], op=ALU.max, axis=AX.X,
                                        negate=True).then_inc(max_ready, 1)
                dve.wait_ge(exp_ready, t + 1)
                nc.vector.reciprocal(inv_sum[:, :], exp_sum[:, :]).then_inc(tile_step, 1)
                nc.vector.scalar_tensor_tensor(out=last_exp[:, :].unsqueeze(1), in0=tile_keys, scalar=LAST_KEY,
                                               in1=expd[:, :].unsqueeze(1), op0=ALU.is_le, op1=ALU.mult,
                                               accum_out=last_exp_sum[:, :]).then_inc(tile_step, 1)
                dve.wait_ge(tile_step, tile_before + 6)
                nc.vector.tensor_tensor(own_exp[:, 0:HISTORY], expd[:, :], last_exp[:, :], ALU.subtract).then_inc(tile_step, 1)
                nc.vector.tensor_scalar(pooled[:, :], last_row[:, :], last_exp_sum[:, :], None, ALU.mult).then_inc(tile_step, 1)
                dve.wait_ge(tile_step, tile_before + 8)
                dve.sem_inc(dve_passed, 1)
                dve.reg_add(base, base, dve.snap(blocks_of(columns)))
                dve.reg_add(pooled_base, pooled_base, dve.snap(blocks_of(columns_before)))

            columns = columns_of(dve, TILES)
            pooled_before = dve.snap(pooled_base, min_val=1, max_val=TILES * BLOCKS + 1)
            with dve.Fori(0, BLOCKS) as v:
                with dve.If(columns > v * BLOCK):
                    pool_block(TILES - 1, v, pooled_before + v)
            nc.vector.tensor_scalar(x_slots[:, TILES:TILES + 1, X_POOL:X_DIM], pooled[:, :].unsqueeze(1), inv_sum[:, :], None,
                                    ALU.mult).then_inc(history_pooled, 1)

            dve.wait_ge(mlp_loaded, MLP_LOADS)
            nc.vector.tensor_scalar(neg_mbias2[:, :], mbias2[:, :], -1.0, None, ALU.mult).then_inc(sigmoid_step, 1)
            for c in range(2):
                dve.wait_ge(xT_ready, 2 * c + 1)
                nc.vector.tensor_copy(xT_lo[:, c * N:(c + 1) * N], p_lo[:, :]).then_inc(xT_copied, 1)
            dve.wait_ge(exp_z, 1)
            nc.vector.tensor_scalar(z[:, :], z[:, :], 1.0, None, ALU.add).then_inc(exp_z, 1)
            dve.wait_ge(exp_z, 2)
            nc.vector.reciprocal(z[:, :], z[:, :]).then_inc(sigmoid_step, 1)


_INS = ['r_user_dense', 'r_user_id', 'r_item_id', 'r_item_category', 'r_item_dur_bkt', 'r_item_dense', 'r_history_seq',
        'L0_rec_user_W', 'L0_rec_item_W', 'L0_rec_cat_W', 'L0_rec_dur_W', 'L0_rec_hist_W',
        'L0_rec_aW0', 'L0_rec_ab0', 'L0_rec_aW1', 'L0_rec_ab1', 'L0_rec_aW2', 'L0_rec_ab2',
        'L0_rec_mW0', 'L0_rec_mb0', 'L0_rec_mW1', 'L0_rec_mb1', 'L0_rec_mW2', 'L0_rec_mb2']


def kernel(**inputs):
    import numpy as np
    import concourse.bacc as bacc
    from concourse import mybir as _mybir
    from concourse.bass_utils import run_bass_kernel_spmd

    nc = bacc.Bacc("TRN2", target_bir_lowering=False, num_devices=1)
    arrays, args = {}, []
    for name in _INS:
        a = np.ascontiguousarray(inputs[name])
        arrays[f"in_{name}"] = a
        args.append(nc.dram_tensor(f"in_{name}", a.shape, _mybir.dt.from_np(a.dtype), kind="ExternalInput").ap())
    batch = inputs['r_history_seq'].shape[0]
    out = nc.dram_tensor("out_0", [batch], _mybir.dt.float32, kind="ExternalOutput").ap()
    build_recommender(nc, *args, out)
    r = run_bass_kernel_spmd(nc, [arrays], core_ids=[0])
    return r.results[0]["out_0"]
```

```python
from contextlib import ExitStack

import concourse.bass as bass
from concourse import mybir

ACT = mybir.ActivationFunctionType
ALU = mybir.AluOpType
AX = mybir.AxisListType
F32 = mybir.dt.float32
I32 = mybir.dt.int32
U32 = mybir.dt.uint32


def build_recommender(
    nc, user_dense, user_id, item_id, item_category, item_dur_bkt, item_dense, history_seq,
    user_W, item_W, cat_W, dur_W, hist_W, aW0, ab0, aW1, ab1, aW2, ab2,
    mW0, mb0, mW1, mb1, mW2, mb2, out,
):
    P = 128
    BATCH, HISTORY = history_seq.shape
    TILES = BATCH // P
    D = hist_W.shape[1]
    LAST = hist_W.shape[0] - 1
    LAST_KEY = float(-LAST)
    A0, A1 = aW0.shape[1], aW1.shape[1]
    UNIT = 8
    SLOTS = 2
    HALF = UNIT // 2
    N = HALF * P
    BLOCK = SLOTS * UNIT
    BLOCKS = -(-HISTORY // BLOCK)
    COLS = BLOCKS * BLOCK
    GROUP = 4
    GROUPS = -(-BLOCKS // GROUP)
    GATHERED = 16 * UNIT
    C_DIM, DUR_DIM = cat_W.shape[1], dur_W.shape[1]
    UD, ID = user_dense.shape[1], item_dense.shape[1]
    X_CAT = 2 * D
    X_DUR = X_CAT + C_DIM
    X_UD = X_DUR + DUR_DIM
    X_ID = X_UD + UD
    X_POOL = X_ID + ID
    X_DIM = X_POOL + D
    M0, M1 = mW0.shape[1], mW1.shape[1]
    X_HI = X_DIM - P
    MASKED = -1000000000.0

    def per_row(ap):
        if len(ap.shape) == 1:
            return ap.rearrange("(p t) -> p t", t=TILES)
        return ap.rearrange("(p t) n -> p t n", t=TILES)

    ctx = ExitStack()
    with ctx:
        def sb(name, shape, dt=F32):
            return ctx.enter_context(nc.sbuf_tensor(name, shape, dt))

        def bank(name):
            return ctx.enter_context(nc.psum_tensor(name, [P, N], F32))

        def sem(name):
            return ctx.enter_context(nc.semaphore(name))

        def slot_sems(name):
            return [sem(f"{name}_{s}") for s in range(SLOTS)]

        ids = sb("ids", [P, 4, TILES], I32)
        ids_f = sb("ids_f", [P, 4, TILES])
        ids_clamped = sb("ids_clamped", [P, 4, TILES], U32)
        history = sb("history", [P, TILES, HISTORY], I32)
        wrapped = sb("wrapped", [P, TILES, HISTORY])
        keys = sb("keys", [P, TILES + 1, HISTORY])
        unsorted = sb("unsorted", [P, HISTORY])
        top = sb("top", [P, SLOTS, UNIT])
        keys_sorted = sb("keys_sorted", [P, TILES + 2, COLS])
        index_sorted = sb("index_sorted", [P, TILES + 1, COLS], U32)
        index_unit = sb("index_unit", [P, SLOTS, UNIT], U32)
        counts = sb("counts", [P, TILES])
        counts_max = sb("counts_max", [TILES, 1])
        needed = sb("needed", [1, TILES + 2], I32)
        needed_most = sb("needed_most", [1, TILES], I32)
        identity = sb("identity", [P, P])
        masked = sb("masked", [P, HISTORY])
        wa = sb("wa", [D, A0])
        wb = sb("wb", [D, A0])
        wd = sb("wd", [D, A0])
        w0 = sb("w0", [2 * D, A0])
        w_item = sb("w_item", [D, 2 * A0])
        b0 = sb("b0", [2 * A0, 1])
        w1 = sb("w1", [2 * A0, 2 * A1])
        b1 = sb("b1", [2 * A1, 1])
        w2 = sb("w2", [2 * A1, 2])
        b2 = sb("b2", [P, 1])
        mw0_lo = sb("mw0_lo", [P, M0])
        mw0_hi = sb("mw0_hi", [X_HI, M0])
        mw1 = sb("mw1", [P, M0 // P, M1])
        mw2 = sb("mw2", [M1, 1])
        mbias0 = sb("mbias0", [P, M0 // P])
        mbias1 = sb("mbias1", [M1, 1])
        mbias2 = sb("mbias2", [P, 1])
        last_row = sb("last_row", [P, D])
        itemT = sb("itemT", [D, TILES * P])
        item_term = sb("item_term", [2 * A0, TILES * P])
        feat = sb("feat", [P, SLOTS, UNIT, 2 * D])
        featT = sb("featT", [2 * D, SLOTS, 2 * N])
        h0 = sb("h0", [2 * A0, SLOTS, N])
        h1 = sb("h1", [2 * A1, SLOTS, N])
        SCORE_COLS = 2 * COLS + UNIT
        scores = sb("scores", [P, SCORE_COLS])
        last_score = sb("last_score", [P, TILES])
        hist = sb("hist", [P, 2, COLS, D])
        tile_scores = sb("tile_scores", [P, HISTORY])
        padding = sb("padding", [P, HISTORY], I32)
        neg_max = sb("neg_max", [P, 1])
        expd = sb("expd", [P, HISTORY])
        exp_sum = sb("exp_sum", [P, 1])
        inv_sum = sb("inv_sum", [P, 1])
        last_exp = sb("last_exp", [P, HISTORY])
        last_exp_sum = sb("last_exp_sum", [P, 1])
        own_exp = sb("own_exp", [P, COLS])
        weighted = sb("weighted", [P, BLOCK, D])
        part = sb("part", [P, D])
        pooled = sb("pooled", [P, D])
        x_slots = sb("x_slots", [P, TILES + 1, X_DIM])
        x = x_slots[:, 1:TILES + 1, :]
        neg_mbias2 = sb("neg_mbias2", [P, 1])
        z = sb("z", [P, TILES])
        spare = hist[:, :, :, :].rearrange("p a c d -> p (a c d)")
        ROWS = TILES * P
        xT_lo = spare[:, 0:ROWS]
        xT_hi = spare[0:X_HI, ROWS:2 * ROWS]
        m0 = [spare[:, (2 + m) * ROWS:(3 + m) * ROWS] for m in range(M0 // P)]
        m1 = spare[:, 4 * ROWS:5 * ROWS]

        p_lo, p_hi = bank("p_lo"), bank("p_hi")
        p_h0 = [bank("p_h0_0"), bank("p_h0_1")]
        p_h1, p_score = bank("p_h1"), bank("p_score")
        p_misc, p_misc2 = bank("p_misc"), bank("p_misc2")

        ids_loaded = sem("ids_loaded")
        history_loaded = sem("history_loaded")
        attention_weights_loaded = sem("attention_weights_loaded")
        mlp_loaded = sem("mlp_loaded")
        weights_cleared = sem("weights_cleared")
        identity_step = sem("identity_step")
        ids_step = sem("ids_step")
        keys_step = sem("keys_step")
        counts_step = sem("counts_step")
        counts_transposed = sem("counts_transposed")
        needed_ready = sem("needed_ready")
        items_landed = sem("items_landed")
        embeddings_landed = sem("embeddings_landed")
        fold_step = sem("fold_step")
        cleared = sem("cleared")
        items_transposed = sem("items_transposed")
        itemT_copied = sem("itemT_copied")
        item_term_summed = sem("item_term_summed")
        item_term_ready = sem("item_term_ready")
        last_feat = sem("last_feat")
        last_transposed = sem("last_transposed")
        last_copied_lo = sem("last_copied_lo")
        last_copied_hi = sem("last_copied_hi")
        last_l0 = sem("last_l0")
        last_added = sem("last_added")
        last_relu0 = sem("last_relu0")
        last_l1 = sem("last_l1")
        last_relu1 = sem("last_relu1")
        last_l2 = sem("last_l2")
        last_scored = sem("last_scored")
        landed = slot_sems("landed")
        index_copied = slot_sems("index_copied")
        pool_passed = sem("pool_passed")
        act_passed = sem("act_passed")
        product_ready = slot_sems("product_ready")
        hist_kept = slot_sems("hist_kept")
        transposed_lo = slot_sems("transposed_lo")
        transposed_hi = slot_sems("transposed_hi")
        copied_lo = slot_sems("copied_lo")
        copied_hi = slot_sems("copied_hi")
        layer0_done = slot_sems("layer0_done")
        item_added = slot_sems("item_added")
        relu0_done = slot_sems("relu0_done")
        layer1_done = slot_sems("layer1_done")
        relu1_done = slot_sems("relu1_done")
        layer2_done = slot_sems("layer2_done")
        scored = slot_sems("scored")
        scores_reset = sem("scores_reset")
        sort_step = sem("sort_step")
        dve_passed = sem("dve_passed")
        block_sorted = sem("block_sorted")
        pool_step = sem("pool_step")
        tile_step = sem("tile_step")
        max_ready = sem("max_ready")
        exp_ready = sem("exp_ready")
        history_pooled = sem("history_pooled")
        xT_ready = sem("xT_ready")
        xT_copied = sem("xT_copied")
        m0_summed = sem("m0_summed")
        m0_ready = sem("m0_ready")
        m1_summed = sem("m1_summed")
        m1_ready = sem("m1_ready")
        m2_summed = sem("m2_summed")
        sigmoid_step = sem("sigmoid_step")
        exp_z = sem("exp_z")
        out_stored = sem("out_stored")

        block = ctx.enter_context(nc.Block())

        def blocks_of(columns):
            return (columns + (BLOCK - 1)) >> 4

        block_registers = {}

        def block_at(eng, group, n):
            eng.reg_mov(block_registers[eng], eng.snap(group * GROUP + n))
            return eng.snap(block_registers[eng], min_val=0, max_val=BLOCKS - 1)

        def item_of(t):
            return x_slots[:, bass.ds(t + 1, 1), D:2 * D]

        def columns_of(eng, t):
            return eng.value_load(needed[0:1, bass.ds(t, 1)], min_val=0, max_val=HISTORY)

        @block.sync
        def _(sp):
            for n, table_ids in enumerate((item_id, user_id, item_category, item_dur_bkt)):
                sp.dma_start(ids[:, n, :], per_row(table_ids)).then_inc(ids_loaded, 16)
            sp.dma_start(history[:, :, :], per_row(history_seq)).then_inc(history_loaded, 16)
            for dst, src in (
                (mw0_lo[:, :], mW0[0:P, :]), (mw0_hi[:, :], mW0[P:X_DIM, :]),
                (mw1[:, :, :], mW1.rearrange("(c p) n -> p c n", p=P)), (mw2[:, :], mW2),
                *((mbias0[:, m:m + 1], mb0[m * P:(m + 1) * P].rearrange("(p a) -> p a", a=1)) for m in range(M0 // P)),
                (mbias1[:, :], mb1.rearrange("(p a) -> p a", a=1)),
                (mbias2[:, :], mb2.rearrange("(p a) -> p a", a=1).broadcast_to([P, 1])),
                (x[:, :, X_UD:X_ID], per_row(user_dense)),
                (x[:, :, X_ID:X_POOL], per_row(item_dense)),
            ):
                sp.dma_start(dst, src).then_inc(mlp_loaded, 16)
            sp.wait_ge(sigmoid_step, 2)
            sp.dma_start(per_row(out), z[:, :]).then_inc(out_stored, 16)
            sp.wait_ge(out_stored, 16)

        MLP_LOADS = 16 * (8 + M0 // P)
        ATTENTION_LOADS = 16 * 14

        @block.gpsimd
        def _(pool):
            for counted in index_copied:
                pool.sem_inc(counted, 1)
            nc.gpsimd.memset(w1[:, :], 0.0).then_inc(weights_cleared, 1)
            nc.gpsimd.memset(w2[:, :], 0.0).then_inc(weights_cleared, 1)
            nc.gpsimd.memset(identity[:, :], 0.0).then_inc(identity_step, 1)
            pool.wait_ge(identity_step, 1)
            nc.gpsimd.affine_select(out=identity[:, :], in_=identity[:, :], compare_op=ALU.not_equal, fill=1.0,
                                    base=0, pattern=[[-1, P]], channel_multiplier=1).then_inc(identity_step, 1)
            pool.wait_ge(ids_step, 3)
            for table, n, at, width, landing in (
                (item_W, 0, D, D, items_landed), (user_W, 1, 0, D, embeddings_landed),
                (cat_W, 2, X_CAT, C_DIM, embeddings_landed), (dur_W, 3, X_DUR, DUR_DIM, embeddings_landed),
            ):
                for t in range(TILES):
                    pool.indirect_dma_start(
                        x[:, t, at:at + width], None, table,
                        bass.IndirectOffsetOnAxis(ap=ids_clamped[:, n, t:t + 1], axis=0),
                    ).then_inc(landing, 16)
                if n == 0:
                    nc.gpsimd.memset(keys_sorted[:, :, :], LAST_KEY).then_inc(cleared, 1)
                    nc.gpsimd.memset(own_exp[:, :], 0.0).then_inc(cleared, 1)
                    nc.gpsimd.memset(masked[:, :], MASKED).then_inc(cleared, 1)
                    nc.gpsimd.memset(pooled[:, :], 0.0).then_inc(cleared, 1)
                    nc.gpsimd.memset(scores[:, :], 0.0).then_inc(cleared, 1)
            pool.wait_ge(needed_ready, 1)
            pool.wait_ge(last_transposed, 2)
            block_registers[pool] = pool.alloc_register("pool_block")
            base = pool.alloc_register("pool_blocks")
            pool.reg_mov(base, 1)
            with pool.Fori(0, TILES) as t:
                columns = columns_of(pool, t + 1)
                before = pool.snap(base, min_val=1, max_val=TILES * BLOCKS + 1)
                with pool.Fori(0, GROUPS) as group:
                    with pool.If(columns > group * (GROUP * BLOCK)):
                        with pool.Fori(0, GROUP) as n:
                            with pool.If(columns > (group * GROUP + n) * BLOCK):
                                v = block_at(pool, group, n)
                                g = before + v
                                pool.wait_ge(block_sorted, g + 1)
                                for s in range(SLOTS):
                                    pool.wait_ge(hist_kept[s], g)
                                    pool.wait_ge(transposed_hi[s], g)
                                    nc.gpsimd.tensor_copy(
                                        index_unit[:, s, :],
                                        index_sorted[:, bass.ds(t, 1), bass.ds(v * BLOCK + s * UNIT, UNIT)]
                                        .rearrange("p a c -> p (a c)"),
                                    ).then_inc(index_copied[s], 1)
                                    pool.wait_ge(index_copied[s], g + 1)
                                    pool.sem_inc(pool_passed, 1)
                                    for k in range(UNIT):
                                        pool.indirect_dma_start(
                                            feat[:, s, k, 0:D], None, hist_W,
                                            bass.IndirectOffsetOnAxis(ap=index_unit[:, s, k:k + 1], axis=0),
                                        ).then_inc(landed[s], 16)
                pool.reg_add(base, base, pool.snap(blocks_of(columns)))

        @block.scalar
        def _(act):
            for counted in (*hist_kept, *copied_hi, *relu0_done, *relu1_done, *scored):
                act.sem_inc(counted, 1)
            loads = [
                (wa[:, :], aW0[0:D, :]), (wb[:, :], aW0[D:2 * D, :]), (w0[D:2 * D, :], aW0[2 * D:3 * D, :]),
                (wd[:, :], aW0[3 * D:4 * D, :]),
                (b2[:, :], ab2.rearrange("(p a) -> p a", a=1).broadcast_to([P, 1])),
                (last_row[:, :], hist_W[LAST:LAST + 1, :].broadcast_to([P, D])),
            ]
            for h in range(2):
                loads += [(b0[h * A0:(h + 1) * A0, :], ab0.rearrange("(p a) -> p a", a=1)),
                          (b1[h * A1:(h + 1) * A1, :], ab1.rearrange("(p a) -> p a", a=1))]
            for h in range(2):
                loads += [(w1[h * A0:(h + 1) * A0, h * A1:(h + 1) * A1], aW1),
                          (w2[h * A1:(h + 1) * A1, h:h + 1], aW2)]
            assert 16 * len(loads) == ATTENTION_LOADS
            for n, (dst, src) in enumerate(loads):
                if n == len(loads) - 4:
                    act.wait_ge(weights_cleared, 2)
                act.dma_start(dst, src).then_inc(attention_weights_loaded, 16)
            act.wait_ge(attention_weights_loaded, ATTENTION_LOADS)

            act.wait_ge(items_transposed, 2)
            nc.scalar.activation(itemT[:, N:2 * N], p_hi[0:D, :], ACT.Copy).then_inc(itemT_copied, 1)
            for c in range(2):
                act.wait_ge(item_term_summed, c + 1)
                nc.scalar.activation(item_term[:, c * N:(c + 1) * N], p_h0[c][:, :], ACT.Identity,
                                     bias=b0[:, :]).then_inc(item_term_ready, 1)
            act.wait_ge(last_transposed, 2)
            nc.scalar.activation(featT[:, 1, N:2 * N], p_hi[:, :], ACT.Copy).then_inc(last_copied_hi, 1)
            act.wait_ge(last_added, 2)
            nc.scalar.activation(h0[:, 1, :], h0[:, 1, :], ACT.Relu).then_inc(last_relu0, 1)
            act.wait_ge(last_l1, 1)
            nc.scalar.activation(h1[:, 1, :], p_h1[0:2 * A1, :], ACT.Relu, bias=b1[:, :]).then_inc(last_relu1, 1)

            act.wait_ge(needed_ready, 1)
            block_registers[act] = act.alloc_register("act_block")
            base = act.alloc_register("act_blocks")
            act.reg_mov(base, 1)
            late_at = act.alloc_register("act_late_scores")
            act.reg_mov(late_at, 2 * COLS)

            def relu1(s, g):
                act.wait_ge(layer2_done[s], g)
                act.wait_ge(layer1_done[s], g + 1)
                nc.scalar.activation(h1[:, s, :], p_h1[0:2 * A1, :], ACT.Relu, bias=b1[:, :]).then_inc(relu1_done[s], 1)

            def put_scores(s, g, at):
                act.wait_ge(layer2_done[s], g + 1)
                nc.scalar.activation(scores[:, bass.ds(at, UNIT)], p_score[:, s * UNIT:(s + 1) * UNIT], ACT.Identity,
                                     bias=b2[:, :]).then_inc(scored[s], 1)

            def exponentials(t):
                act.wait_ge(max_ready, t + 1)
                nc.scalar.activation(expd[:, :], tile_scores[:, :], ACT.Exp,
                                     bias=neg_max[:, :], accum_out=exp_sum[:, :]).then_inc(exp_ready, 1)

            with act.Fori(0, TILES) as t:
                columns = columns_of(act, t + 1)
                before = act.snap(base, min_val=1, max_val=TILES * BLOCKS + 1)
                act.wait_ge(history_pooled, t + 1)
                act.sem_inc(act_passed, 1)
                act.wait_ge(scores_reset, t + 1)
                act.sem_inc(act_passed, 1)
                with act.Fori(0, GROUPS) as group:
                    with act.If(columns > group * (GROUP * BLOCK)):
                        with act.Fori(0, GROUP) as n:
                            with act.If(columns > (group * GROUP + n) * BLOCK):
                                v = block_at(act, group, n)
                                g = before + v
                                for s in range(SLOTS):
                                    act.wait_ge(landed[s], g * GATHERED)
                                    nc.scalar.activation(
                                        hist[:, bass.ds(t & 1, 1), bass.ds(v * BLOCK + s * UNIT, UNIT), :]
                                        .rearrange("p a c d -> p (a c) d"),
                                        feat[:, s, :, 0:D], ACT.Copy).then_inc(hist_kept[s], 1)
                                    act.wait_ge(transposed_hi[s], g + 1)
                                    nc.scalar.activation(featT[:, s, N:2 * N], p_hi[:, :], ACT.Copy).then_inc(copied_hi[s], 1)
                                    relu1(1 - s, g)
                                    if s == 1:
                                        with act.If(v == 0):
                                            exponentials(t)
                                    act.wait_ge(item_added[s], g + 1)
                                    nc.scalar.activation(h0[:, s, :], h0[:, s, :], ACT.Relu).then_inc(relu0_done[s], 1)
                                    if s == 0:
                                        put_scores(1, g, act.snap(late_at, min_val=0, max_val=SCORE_COLS - UNIT))
                                    else:
                                        put_scores(0, g, (t & 1) * COLS + v * BLOCK)
                                        act.reg_mov(late_at, act.snap((t & 1) * COLS + v * BLOCK + UNIT))
                act.reg_add(base, base, act.snap(blocks_of(columns)))
            g = act.snap(base, min_val=1, max_val=TILES * BLOCKS + 1)
            relu1(1, g)
            put_scores(1, g, act.snap(late_at, min_val=0, max_val=SCORE_COLS - UNIT))
            exponentials(TILES)

            act.wait_ge(mlp_loaded, MLP_LOADS)
            for c in range(2):
                act.wait_ge(xT_ready, 2 * c + 2)
                nc.scalar.activation(xT_hi[:, c * N:(c + 1) * N], p_hi[0:X_HI, :], ACT.Copy).then_inc(xT_copied, 1)
            for c in range(2):
                for m in range(M0 // P):
                    act.wait_ge(m0_summed, 2 * c + m + 1)
                    nc.scalar.activation(m0[m][:, c * N:(c + 1) * N], p_h0[m][:, :], ACT.Relu,
                                         bias=mbias0[:, m:m + 1]).then_inc(m0_ready, 1)
                act.wait_ge(m1_summed, c + 1)
                nc.scalar.activation(m1[:, c * N:(c + 1) * N], p_h1[:, :], ACT.Relu,
                                     bias=mbias1[:, :]).then_inc(m1_ready, 1)
            act.wait_ge(m2_summed, 1)
            act.wait_ge(sigmoid_step, 0 + 1)
            nc.scalar.activation(z[:, :], p_misc[:, 0:TILES], ACT.Exp, scale=-1.0,
                                 bias=neg_mbias2[:, :]).then_inc(exp_z, 1)

        @block.tensor
        def _(pe):
            for counted in (*transposed_lo, *transposed_hi, *layer0_done, *layer1_done, *layer2_done):
                pe.sem_inc(counted, 1)
            pe.wait_ge(identity_step, 2)
            pe.wait_ge(counts_step, 1)
            nc.tensor.transpose(p_misc[0:TILES, 0:P], counts[:, :], identity[:, :]).then_inc(counts_transposed, 1)
            pe.wait_ge(counts_step, 2)
            nc.tensor.matmul(p_misc2[0:1, 0:TILES], counts_max[:, :], identity[0:TILES, 0:TILES],
                             start=True, stop=True).then_inc(counts_transposed, 1)
            pe.wait_ge(items_landed, 16 * TILES)
            for c, dst in enumerate((p_lo, p_hi)):
                for k in range(HALF):
                    last = nc.tensor.transpose(dst[0:D, k * P:(k + 1) * P], x[:, c * HALF + k, D:2 * D], identity[:, :])
                last.then_inc(items_transposed, 1)
            pe.wait_ge(fold_step, 3)
            pe.wait_ge(itemT_copied, 2)
            for c in range(2):
                nc.tensor.matmul(p_h0[c][:, :], w_item[:, :], itemT[:, c * N:(c + 1) * N],
                                 start=True, stop=True).then_inc(item_term_summed, 1)
            pe.wait_ge(last_feat, 2)
            for c, dst in enumerate((p_lo, p_hi)):
                for k in range(HALF):
                    last = nc.tensor.transpose(dst[:, k * P:(k + 1) * P], feat[:, 1, c * HALF + k, :], identity[:, :])
                last.then_inc(last_transposed, 1)
            pe.wait_ge(last_copied_lo, 1)
            pe.wait_ge(item_term_ready, 2)
            nc.tensor.matmul(p_h0[1][0:A0, :], w0[:, :], featT[:, 1, 0:N], start=True, stop=True)
            pe.wait_ge(last_copied_hi, 1)
            nc.tensor.matmul(p_h0[1][A0:2 * A0, :], w0[:, :], featT[:, 1, N:2 * N],
                             start=True, stop=True).then_inc(last_l0, 1)
            pe.wait_ge(last_relu0, 1)
            nc.tensor.matmul(p_h1[0:2 * A1, :], w1[:, :], h0[:, 1, :], start=True, stop=True).then_inc(last_l1, 1)
            pe.wait_ge(last_relu1, 1)
            for k in range(HALF):
                last = nc.tensor.matmul(p_score[:, k:UNIT:HALF], h1[:, 1, k * P:(k + 1) * P], w2[:, :],
                                        start=True, stop=True)
            last.then_inc(last_l2, 1)
            pe.wait_ge(last_scored, 1)

            pe.wait_ge(needed_ready, 1)
            block_registers[pe] = pe.alloc_register("pe_block")
            base = pe.alloc_register("pe_blocks")
            pe.reg_mov(base, 1)
            def layer1(s, g):
                pe.wait_ge(relu1_done[1 - s], g if s == 1 else g + 1)
                pe.wait_ge(relu0_done[s], g if s == 1 else g + 1)
                nc.tensor.matmul(p_h1[0:2 * A1, :], w1[:, :], h0[:, s, :], start=True, stop=True).then_inc(layer1_done[s], 1)

            def layer2(s, g):
                pe.wait_ge(scored[s], g)
                pe.wait_ge(relu1_done[s], g + 1)
                for k in range(HALF):
                    last = nc.tensor.matmul(p_score[:, s * UNIT + k:(s + 1) * UNIT:HALF],
                                            h1[:, s, k * P:(k + 1) * P], w2[:, :], start=True, stop=True)
                last.then_inc(layer2_done[s], 1)

            with pe.Fori(0, TILES) as t:
                columns = columns_of(pe, t + 1)
                before = pe.snap(base, min_val=1, max_val=TILES * BLOCKS + 1)
                with pe.Fori(0, GROUPS) as group:
                    with pe.If(columns > group * (GROUP * BLOCK)):
                        with pe.Fori(0, GROUP) as n:
                            with pe.If(columns > (group * GROUP + n) * BLOCK):
                                g = before + block_at(pe, group, n)
                                for s in range(SLOTS):
                                    pe.wait_ge(product_ready[s], g + 1)
                                    pe.wait_ge(copied_lo[1 - s], g + s)
                                    for k in range(HALF):
                                        last = nc.tensor.transpose(p_lo[:, k * P:(k + 1) * P], feat[:, s, k, :],
                                                                   identity[:, :])
                                    last.then_inc(transposed_lo[s], 1)
                                    pe.wait_ge(copied_hi[1 - s], g + s)
                                    for k in range(HALF):
                                        last = nc.tensor.transpose(p_hi[:, k * P:(k + 1) * P], feat[:, s, HALF + k, :],
                                                                   identity[:, :])
                                    last.then_inc(transposed_hi[s], 1)
                                    layer1(1 - s, g)
                                    pe.wait_ge(item_added[s], g)
                                    pe.wait_ge(copied_lo[s], g + 1)
                                    nc.tensor.matmul(p_h0[s][0:A0, :], w0[:, :], featT[:, s, 0:N], start=True, stop=True)
                                    pe.wait_ge(copied_hi[s], g + 1)
                                    nc.tensor.matmul(p_h0[s][A0:2 * A0, :], w0[:, :], featT[:, s, N:2 * N],
                                                     start=True, stop=True).then_inc(layer0_done[s], 1)
                                    layer2(1 - s, g)
                pe.reg_add(base, base, pe.snap(blocks_of(columns)))
            g = pe.snap(base, min_val=1, max_val=TILES * BLOCKS + 1)
            layer1(1, g)
            layer2(1, g)

            pe.wait_ge(mlp_loaded, MLP_LOADS)
            pe.wait_ge(embeddings_landed, 3 * 16 * TILES)
            pe.wait_ge(history_pooled, TILES + 2)
            for c in range(2):
                if c:
                    pe.wait_ge(xT_copied, 2 * c)
                for k in range(HALF):
                    last = nc.tensor.transpose(p_lo[:, k * P:(k + 1) * P], x[:, c * HALF + k, 0:P], identity[:, :])
                last.then_inc(xT_ready, 1)
                for k in range(HALF):
                    last = nc.tensor.transpose(p_hi[0:X_HI, k * P:(k + 1) * P], x[:, c * HALF + k, P:X_DIM],
                                               identity[:, :])
                last.then_inc(xT_ready, 1)
            for c in range(2):
                rows = slice(c * N, (c + 1) * N)
                if c == 0:
                    pe.wait_ge(xT_copied, 4)
                for m in range(M0 // P):
                    if c:
                        pe.wait_ge(m0_ready, m + 1)
                    nc.tensor.matmul(p_h0[m][:, :], mw0_lo[:, m * P:(m + 1) * P], xT_lo[:, rows], start=True, stop=False)
                    nc.tensor.matmul(p_h0[m][:, :], mw0_hi[:, m * P:(m + 1) * P], xT_hi[:, rows],
                                     start=False, stop=True).then_inc(m0_summed, 1)
                if c:
                    pe.wait_ge(m1_ready, c)
                for m in range(M0 // P):
                    pe.wait_ge(m0_ready, 2 * c + m + 1)
                    last = nc.tensor.matmul(p_h1[:, :], mw1[:, m, :], m0[m][:, rows], start=(m == 0),
                                            stop=(m == M0 // P - 1))
                last.then_inc(m1_summed, 1)
            pe.wait_ge(m1_ready, 2)
            for t in range(TILES):
                last = nc.tensor.matmul(p_misc[:, t:t + 1], m1[:, t * P:(t + 1) * P], mw2[:, :], start=True, stop=True)
            last.then_inc(m2_summed, 1)

        @block.vector
        def _(dve):
            for counted in (*product_ready, *copied_lo, *item_added, block_sorted, history_pooled):
                dve.sem_inc(counted, 1)
            dve.sem_inc(sort_step, 4)
            dve.sem_inc(pool_step, 3)
            dve.wait_ge(ids_loaded, 16 * 4)
            tables = (item_W, user_W, cat_W, dur_W)
            for n, table in enumerate(tables):
                last = nc.vector.tensor_scalar(ids_f[:, n, :], ids[:, n, :], 0.0, float(table.shape[0]), ALU.is_lt, ALU.mult)
            last.then_inc(ids_step, 1)
            dve.wait_ge(ids_step, 1)
            nc.vector.tensor_tensor(ids_f[:, :, :], ids_f[:, :, :], ids[:, :, :], ALU.add).then_inc(ids_step, 1)
            dve.wait_ge(ids_step, 2)
            for n, table in enumerate(tables):
                last = nc.vector.tensor_scalar(ids_clamped[:, n, :], ids_f[:, n, :], 0.0, float(table.shape[0] - 1),
                                               ALU.max, ALU.min)
            last.then_inc(ids_step, 1)
            nc.vector.memset(keys[:, TILES, :], LAST_KEY).then_inc(keys_step, 1)
            nc.vector.memset(needed[:, :], 0).then_inc(keys_step, 1)
            dve.wait_ge(history_loaded, 16)
            nc.vector.tensor_scalar(wrapped[:, :, :], history[:, :, :], 0.0, float(LAST + 1), ALU.is_lt,
                                    ALU.mult).then_inc(keys_step, 1)
            dve.wait_ge(keys_step, 3)
            nc.vector.tensor_tensor(wrapped[:, :, :], wrapped[:, :, :], history[:, :, :], ALU.add).then_inc(keys_step, 1)
            dve.wait_ge(keys_step, 4)
            nc.vector.tensor_scalar(wrapped[:, :, :], wrapped[:, :, :], 0.0, float(LAST), ALU.max,
                                    ALU.min).then_inc(keys_step, 1)
            dve.wait_ge(keys_step, 5)
            nc.vector.scalar_tensor_tensor(out=keys[:, 0:TILES, :], in0=history[:, :, :], scalar=0.0,
                                           in1=wrapped[:, :, :], op0=ALU.is_equal, op1=ALU.subtract).then_inc(keys_step, 1)
            dve.wait_ge(keys_step, 6)
            for t in range(TILES):
                last = nc.vector.tensor_scalar(wrapped[:, t, :], keys[:, t, :], LAST_KEY, 0.0, ALU.is_gt, ALU.add,
                                               accum_out=counts[:, t:t + 1])
            last.then_inc(counts_step, 1)
            dve.wait_ge(counts_transposed, 1)
            nc.vector.reduce_max(counts_max[:, :], p_misc[0:TILES, 0:P], AX.X).then_inc(counts_step, 1)
            dve.wait_ge(counts_transposed, 2)
            nc.vector.tensor_scalar(needed[:, 1:TILES + 1], p_misc2[0:1, 0:TILES], 1.0, None, ALU.max).then_inc(needed_ready, 1)
            dve.wait_ge(needed_ready, 1)
            nc.vector.tensor_tensor(needed_most[:, :], needed[:, 0:TILES], needed[:, 1:TILES + 1], ALU.max).then_inc(counts_step, 1)
            dve.wait_ge(counts_step, 3)
            nc.vector.tensor_tensor(needed_most[:, :], needed_most[:, :], needed[:, 2:TILES + 2], ALU.max).then_inc(counts_step, 1)
            dve.wait_ge(counts_step, 4)

            def load_keys(t):
                return nc.vector.tensor_copy(unsorted[:, :].unsqueeze(1), keys[:, bass.ds(t, 1), :])

            def sort_block(t, v, sorted_before):
                dve.wait_ge(block_sorted, sorted_before)
                for s in range(SLOTS):
                    dve.wait_ge(sort_step, sorted_before * 4 + 2 * s)
                    dve.sem_inc(dve_passed, 1)
                    nc.vector.max(out=top[:, s, :], in_=unsorted[:, :]).then_inc(sort_step, 1)
                    dve.wait_ge(sort_step, sorted_before * 4 + 2 * s + 1)
                    dve.sem_inc(dve_passed, 1)
                    nc.vector.match_replace(out=unsorted[:, :], in_to_replace=top[:, s, :], in_values=unsorted[:, :],
                                            imm_value=LAST_KEY).then_inc(sort_step, 1)
                columns = bass.ds(v * BLOCK, BLOCK)
                found = top[:, :, :].rearrange("p s c -> p (s c)").unsqueeze(1)
                nc.vector.tensor_copy(keys_sorted[:, bass.ds(t + 1, 1), columns], found)
                nc.vector.tensor_scalar(index_sorted[:, bass.ds(t, 1), columns], found, -1.0, 0.0, ALU.mult,
                                        ALU.max).then_inc(block_sorted, 1)

            def pool_block(t, v, pooled_before):
                columns = bass.ds(v * BLOCK, BLOCK)
                for s in range(SLOTS):
                    dve.wait_ge(hist_kept[s], pooled_before + 1)
                nc.vector.tensor_tensor(
                    weighted[:, :, :], hist[:, bass.ds(t & 1, 1), columns, :].rearrange("p a c d -> p (a c) d"),
                    own_exp[:, columns].unsqueeze(2).broadcast_to([P, BLOCK, D]), ALU.mult).then_inc(pool_step, 1)
                dve.wait_ge(pool_step, pooled_before * 3 + 1)
                nc.vector.tensor_reduce(part[:, :], weighted[:, :, :].rearrange("p c d -> p d c"), op=ALU.add,
                                        axis=AX.X).then_inc(pool_step, 1)
                dve.wait_ge(pool_step, pooled_before * 3 + 2)
                nc.vector.tensor_tensor(pooled[:, :], pooled[:, :], part[:, :], ALU.add).then_inc(pool_step, 1)
                dve.wait_ge(pool_step, pooled_before * 3 + 3)
                dve.sem_inc(dve_passed, 1)

            columns0 = columns_of(dve, 1)
            dve.wait_ge(cleared, 5)
            load_keys(0).then_inc(keys_step, 1)
            dve.wait_ge(keys_step, 7)
            with dve.Fori(0, BLOCKS) as v:
                with dve.If(columns0 > v * BLOCK):
                    sort_block(0, v, v + 1)

            dve.wait_ge(attention_weights_loaded, ATTENTION_LOADS)
            nc.vector.tensor_tensor(w0[0:D, :], wa[:, :], wd[:, :], ALU.add).then_inc(fold_step, 1)
            for h in range(2):
                nc.vector.tensor_tensor(w_item[:, h * A0:(h + 1) * A0], wb[:, :], wd[:, :],
                                        ALU.subtract).then_inc(fold_step, 1)
            dve.wait_ge(items_transposed, 1)
            nc.vector.tensor_copy(itemT[:, 0:N], p_lo[0:D, :]).then_inc(itemT_copied, 1)
            last_rows = last_row[:, :].unsqueeze(1).broadcast_to([P, TILES, D])
            nc.vector.tensor_copy(feat[:, 1, :, 0:D], last_rows).then_inc(last_feat, 1)
            dve.wait_ge(items_landed, 16 * TILES)
            nc.vector.tensor_tensor(feat[:, 1, :, D:2 * D], last_rows, x[:, :, D:2 * D], ALU.mult).then_inc(last_feat, 1)
            dve.wait_ge(last_transposed, 1)
            nc.vector.tensor_copy(featT[:, 1, 0:N], p_lo[:, :]).then_inc(last_copied_lo, 1)
            dve.wait_ge(last_l0, 1)
            for h in range(2):
                part_rows = slice(h * A0, (h + 1) * A0)
                nc.vector.tensor_tensor(h0[part_rows, 1, :], p_h0[1][part_rows, :], item_term[part_rows, h * N:(h + 1) * N],
                                        ALU.add).then_inc(last_added, 1)
            dve.wait_ge(last_l2, 1)
            nc.vector.tensor_scalar(last_score[:, :], p_score[:, 0:TILES], b2[:, :], None, ALU.add).then_inc(last_scored, 1)
            dve.wait_ge(last_scored, 1)

            block_registers[dve] = dve.alloc_register("dve_block")
            base = dve.alloc_register("dve_blocks")
            dve.reg_mov(base, 1)
            pooled_base = dve.alloc_register("dve_blocks_pooled")
            dve.reg_mov(pooled_base, 1)
            TILE_STEPS = 8

            def softmax(t, steps_before):
                tile_keys = keys_sorted[:, bass.ds(t, 1), 0:HISTORY]
                nc.vector.tensor_copy(tile_scores[:, :], scores[:, bass.ds(((t + 1) & 1) * COLS, HISTORY)]).then_inc(tile_step, 1)
                nc.vector.tensor_scalar(padding[:, :].unsqueeze(1), tile_keys, 0.5, None, ALU.is_gt).then_inc(tile_step, 1)
                dve.wait_ge(tile_step, steps_before + 3)
                dve.sem_inc(dve_passed, 1)
                nc.vector.copy_predicated(tile_scores[:, :], padding[:, :], masked[:, :]).then_inc(tile_step, 1)
                dve.wait_ge(tile_step, steps_before + 4)
                nc.vector.tensor_reduce(neg_max[:, :], tile_scores[:, :], op=ALU.max, axis=AX.X, negate=True).then_inc(max_ready, 1)
                dve.wait_ge(exp_ready, t + 1)
                nc.vector.reciprocal(inv_sum[:, :], exp_sum[:, :]).then_inc(tile_step, 1)
                nc.vector.scalar_tensor_tensor(out=last_exp[:, :].unsqueeze(1), in0=tile_keys, scalar=LAST_KEY,
                                               in1=expd[:, :].unsqueeze(1), op0=ALU.is_le, op1=ALU.mult,
                                               accum_out=last_exp_sum[:, :]).then_inc(tile_step, 1)
                dve.wait_ge(tile_step, steps_before + 6)
                nc.vector.tensor_tensor(own_exp[:, 0:HISTORY], expd[:, :], last_exp[:, :], ALU.subtract).then_inc(tile_step, 1)
                nc.vector.tensor_scalar(pooled[:, :], last_row[:, :], last_exp_sum[:, :], None, ALU.mult).then_inc(tile_step, 1)
                dve.wait_ge(tile_step, steps_before + 8)
                dve.sem_inc(dve_passed, 1)

            def finish_pooling(t):
                nc.vector.tensor_scalar(x_slots[:, bass.ds(t, 1), X_POOL:X_DIM], pooled[:, :].unsqueeze(1),
                                        inv_sum[:, :], None, ALU.mult).then_inc(history_pooled, 1)

            with dve.Fori(0, TILES) as t:
                columns_before = columns_of(dve, t)
                columns = columns_of(dve, t + 1)
                columns_next = columns_of(dve, t + 2)
                columns_most = dve.value_load(needed_most[0:1, bass.ds(t, 1)], min_val=0, max_val=HISTORY)
                before = dve.snap(base, min_val=1, max_val=TILES * BLOCKS + 1)
                sorted_before = dve.snap(before + blocks_of(columns))
                pooled_before = dve.snap(pooled_base, min_val=1, max_val=TILES * BLOCKS + 1)
                steps_before = dve.snap(t * TILE_STEPS)
                dve.wait_ge(sort_step, sorted_before * 4)
                load_keys(t + 1).then_inc(tile_step, 1)
                nc.vector.tensor_copy(scores[:, bass.ds((t & 1) * COLS, COLS)],
                                      last_score[:, bass.ds(t, 1)].broadcast_to([P, COLS])).then_inc(scores_reset, 1)
                dve.wait_ge(tile_step, steps_before + 1)
                dve.sem_inc(dve_passed, 1)
                with dve.Fori(0, GROUPS) as group:
                    with dve.If(columns_most > group * (GROUP * BLOCK)):
                        with dve.Fori(0, GROUP) as n:
                            start = dve.snap((group * GROUP + n) * BLOCK)
                            with dve.If(columns > start):
                                v = block_at(dve, group, n)
                                g = before + v
                                for s in range(SLOTS):
                                    dve.wait_ge(landed[s], g * GATHERED)
                                    nc.vector.tensor_tensor(feat[:, s, :, D:2 * D], feat[:, s, :, 0:D],
                                                            item_of(t).broadcast_to([P, UNIT, D]),
                                                            ALU.mult).then_inc(product_ready[s], 1)
                                    dve.wait_ge(transposed_lo[s], g + 1)
                                    nc.vector.tensor_copy(featT[:, s, 0:N], p_lo[:, :]).then_inc(copied_lo[s], 1)
                                    if s == 0:
                                        with dve.If(columns_next > start):
                                            sort_block(t + 1, v, sorted_before + v)
                                    else:
                                        with dve.If(v == 0):
                                            dve.wait_ge(scored[1], before + 1)
                                            softmax(t, steps_before)
                                        with dve.If(columns_before > start):
                                            pool_block(t + 1, v, pooled_before + v)
                                    dve.wait_ge(layer1_done[s], g + s)
                                    dve.wait_ge(layer0_done[s], g + 1)
                                    nc.vector.tensor_tensor(
                                        h0[:, s, :].rearrange("p (k b) -> p k b", k=HALF),
                                        p_h0[s][:, :].rearrange("p (k b) -> p k b", k=HALF),
                                        item_term[:, bass.ds(t * P, P)].unsqueeze(1).broadcast_to([P, HALF, P]),
                                        ALU.add).then_inc(item_added[s], 1)
                            with dve.Else():
                                with dve.If(columns_next > start):
                                    v = block_at(dve, group, n)
                                    sort_block(t + 1, v, sorted_before + v)
                                with dve.If(columns_before > start):
                                    v = block_at(dve, group, n)
                                    pool_block(t + 1, v, pooled_before + v)
                                dve.sem_inc(dve_passed, 1)
                finish_pooling(t)
                dve.wait_ge(history_pooled, t + 2)
                dve.sem_inc(dve_passed, 1)
                dve.reg_add(base, base, dve.snap(blocks_of(columns)))
                dve.reg_add(pooled_base, pooled_base, dve.snap(blocks_of(columns_before)))

            columns = columns_of(dve, TILES)
            blocks_done = dve.snap(base, min_val=1, max_val=TILES * BLOCKS + 1)
            pooled_before = dve.snap(pooled_base, min_val=1, max_val=TILES * BLOCKS + 1)
            dve.wait_ge(scored[0], blocks_done)
            dve.wait_ge(scored[1], blocks_done + 1)
            softmax(TILES, TILES * TILE_STEPS - 1)
            with dve.Fori(0, BLOCKS) as v:
                with dve.If(columns > v * BLOCK):
                    pool_block(TILES - 1, v, pooled_before + v)
            finish_pooling(TILES)

            dve.wait_ge(mlp_loaded, MLP_LOADS)
            nc.vector.tensor_scalar(neg_mbias2[:, :], mbias2[:, :], -1.0, None, ALU.mult).then_inc(sigmoid_step, 1)
            for c in range(2):
                dve.wait_ge(xT_ready, 2 * c + 1)
                nc.vector.tensor_copy(xT_lo[:, c * N:(c + 1) * N], p_lo[:, :]).then_inc(xT_copied, 1)
            dve.wait_ge(exp_z, 1)
            nc.vector.tensor_scalar(z[:, :], z[:, :], 1.0, None, ALU.add).then_inc(exp_z, 1)
            dve.wait_ge(exp_z, 2)
            nc.vector.reciprocal(z[:, :], z[:, :]).then_inc(sigmoid_step, 1)


_INS = ['r_user_dense', 'r_user_id', 'r_item_id', 'r_item_category', 'r_item_dur_bkt', 'r_item_dense', 'r_history_seq',
        'L0_rec_user_W', 'L0_rec_item_W', 'L0_rec_cat_W', 'L0_rec_dur_W', 'L0_rec_hist_W',
        'L0_rec_aW0', 'L0_rec_ab0', 'L0_rec_aW1', 'L0_rec_ab1', 'L0_rec_aW2', 'L0_rec_ab2',
        'L0_rec_mW0', 'L0_rec_mb0', 'L0_rec_mW1', 'L0_rec_mb1', 'L0_rec_mW2', 'L0_rec_mb2']


def kernel(**inputs):
    import numpy as np
    import concourse.bacc as bacc
    from concourse import mybir as _mybir
    from concourse.bass_utils import run_bass_kernel_spmd

    nc = bacc.Bacc("TRN2", target_bir_lowering=False, num_devices=1)
    arrays, args = {}, []
    for name in _INS:
        a = np.ascontiguousarray(inputs[name])
        arrays[f"in_{name}"] = a
        args.append(nc.dram_tensor(f"in_{name}", a.shape, _mybir.dt.from_np(a.dtype), kind="ExternalInput").ap())
    batch = inputs['r_history_seq'].shape[0]
    out = nc.dram_tensor("out_0", [batch], _mybir.dt.float32, kind="ExternalOutput").ap()
    build_recommender(nc, *args, out)
    r = run_bass_kernel_spmd(nc, [arrays], core_ids=[0])
    return r.results[0]["out_0"]
```

```python
from contextlib import ExitStack

import concourse.bass as bass
from concourse import mybir

ACT = mybir.ActivationFunctionType
ALU = mybir.AluOpType
AX = mybir.AxisListType
F32 = mybir.dt.float32
I32 = mybir.dt.int32
U32 = mybir.dt.uint32


def build_recommender(
    nc, user_dense, user_id, item_id, item_category, item_dur_bkt, item_dense, history_seq,
    user_W, item_W, cat_W, dur_W, hist_W, aW0, ab0, aW1, ab1, aW2, ab2,
    mW0, mb0, mW1, mb1, mW2, mb2, out,
):
    P = 128
    BATCH, HISTORY = history_seq.shape
    TILES = BATCH // P
    D = hist_W.shape[1]
    LAST = hist_W.shape[0] - 1
    LAST_KEY = float(-LAST)
    A0, A1 = aW0.shape[1], aW1.shape[1]
    UNIT = 8
    SLOTS = 2
    HALF = UNIT // 2
    N = HALF * P
    BLOCK = SLOTS * UNIT
    BLOCKS = -(-HISTORY // BLOCK)
    COLS = BLOCKS * BLOCK
    HEAD = 4
    LEAST = (HEAD - 1) * BLOCK
    REST_GROUP = 3
    REST_GROUPS = -(-(BLOCKS - HEAD) // REST_GROUP)
    REST_START = HEAD * BLOCK
    C_DIM, DUR_DIM = cat_W.shape[1], dur_W.shape[1]
    UD, ID = user_dense.shape[1], item_dense.shape[1]
    X_UD = 2 * D
    X_ID = X_UD + UD
    X_POOL = X_ID + ID
    X_DIM = X_POOL + D
    X_IDS = X_DIM
    M0, M1 = mW0.shape[1], mW1.shape[1]
    X_HI = X_DIM - P
    CD_AT = -(-X_HI // 32) * 32
    CD = C_DIM + DUR_DIM
    X_K = CD_AT + CD
    ACT_COUNTS = TILES // 2
    LAG = 2
    CAT_CHUNKS = -(-cat_W.shape[0] // P)
    CHUNKS = CAT_CHUNKS + 1
    MASKED = -1000000000.0

    def per_row(ap):
        if len(ap.shape) == 1:
            return ap.rearrange("(p t) -> p t", t=TILES)
        return ap.rearrange("(p t) n -> p t n", t=TILES)

    ctx = ExitStack()
    with ctx:
        def sb(name, shape, dt=F32):
            return ctx.enter_context(nc.sbuf_tensor(name, shape, dt))

        def bank(name):
            return ctx.enter_context(nc.psum_tensor(name, [P, N], F32))

        def sem(name):
            return ctx.enter_context(nc.semaphore(name))

        def slot_sems(name):
            return [sem(f"{name}_{s}") for s in range(SLOTS)]

        ids = sb("ids", [P, 4, TILES], I32)
        ids_f = sb("ids_f", [P, 4, TILES])
        ids_clamped = sb("ids_clamped", [P, 2, TILES], U32)
        history = sb("history", [P, TILES, HISTORY], I32)
        wrapped = sb("wrapped", [P, TILES, HISTORY])
        keys = sb("keys", [P, TILES, HISTORY])
        keys_next = sb("keys_next", [P, HISTORY])
        unsorted = sb("unsorted", [P, HISTORY])
        top = sb("top", [P, SLOTS, UNIT])
        keys_sorted = sb("keys_sorted", [P, TILES + 2, COLS])
        index_head = sb("index_head", [P, HEAD, BLOCK], U32)
        index_rest = sb("index_rest", [P, BLOCK], U32)
        index_rest_sorted = sb("index_rest_sorted", [P, 2, COLS - REST_START], U32)
        sign_bias = sb("sign_bias", [P, 1])
        sign_sums = sb("sign_sums", [P, ACT_COUNTS])
        counts = sb("counts", [P, TILES])
        numbers_i = sb("numbers_i", [P, 2, TILES], I32)
        numbers = sb("numbers", [P, 2, TILES])
        rank_by = sb("rank_by", [P, TILES])
        beats = sb("beats", [P, TILES, TILES])
        rank = sb("rank", [P, TILES])
        row_of = sb("row_of", [P, TILES + LAG + 2, TILES])
        ids_picked = sb("ids_picked", [P, 4, TILES])
        counts_picked = sb("counts_picked", [P, TILES])
        own_most = sb("own_most", [1, TILES], I32)
        counts_max = sb("counts_max", [TILES, 1])
        needed = sb("needed", [1, TILES + 3], I32)
        needed_most = sb("needed_most", [1, TILES + 1], I32)
        identity = sb("identity", [P, P])
        masked = sb("masked", [P, HISTORY])
        wa = sb("wa", [D, A0])
        wb = sb("wb", [D, A0])
        wd = sb("wd", [D, A0])
        w0 = sb("w0", [2 * D, A0])
        w_item = sb("w_item", [D, 2 * A0])
        b0 = sb("b0", [2 * A0, 1])
        w1 = sb("w1", [2 * A0, 2 * A1])
        b1 = sb("b1", [2 * A1, 1])
        w2 = sb("w2", [2 * A1, 2])
        b2 = sb("b2", [P, 1])
        mw0_lo = sb("mw0_lo", [P, M0])
        mw0_hi = sb("mw0_hi", [X_K, M0])
        mw1 = sb("mw1", [P, M0 // P, M1])
        mw2 = sb("mw2", [M1, 1])
        mbias0 = sb("mbias0", [P, M0 // P])
        mbias1 = sb("mbias1", [M1, 1])
        mbias2 = sb("mbias2", [P, 1])
        last_row = sb("last_row", [P, D])
        item_term = sb("item_term", [2 * A0, TILES * P])
        feat = sb("feat", [P, 2, SLOTS, UNIT, 2 * D])
        featT = sb("featT", [2 * D, SLOTS, 2 * N])
        h0 = sb("h0", [2 * A0, SLOTS, N])
        h1 = sb("h1", [2 * A1, SLOTS, N])
        SCORE_COLS = 2 * COLS + UNIT
        scores = sb("scores", [P, SCORE_COLS])
        last_score = sb("last_score", [P, TILES])
        hist = sb("hist", [P, 2, COLS, D])
        tile_scores = sb("tile_scores", [P, HISTORY])
        padding = sb("padding", [P, HISTORY], I32)
        neg_max = sb("neg_max", [P, 1])
        expd = sb("expd", [P, HISTORY])
        exp_sum = sb("exp_sum", [P, 1])
        inv_sum = sb("inv_sum", [P, 1])
        last_exp = sb("last_exp", [P, HISTORY])
        last_exp_sum = sb("last_exp_sum", [P, 1])
        own_exp = sb("own_exp", [P, COLS])
        weighted = sb("weighted", [P, BLOCK, D])
        part = sb("part", [P, D])
        pooled = sb("pooled", [P, D])
        x_slots = sb("x_slots", [P, TILES + LAG, 2 * D + 2])
        x = x_slots[:, LAG:, :]
        x_rows = sb("x_rows", [P, TILES, D + UD + ID])
        x_now = sb("x_now", [P, X_DIM + 2])
        ones = sb("ones", [P, P])
        row_numbers_i = sb("row_numbers_i", [P, CAT_CHUNKS], I32)
        row_numbers = sb("row_numbers", [P, CAT_CHUNKS])
        cd_rows = sb("cd_rows", [P, CHUNKS, CD])
        ids_diagonal = sb("ids_diagonal", [P, 2, P])
        one_hot = sb("one_hot", [P, CHUNKS, P])
        xT_lo = sb("xT_lo", [P, P])
        xT_hi = sb("xT_hi", [X_K, P])
        m0 = sb("m0", [P, M0 // P, P])
        m1 = sb("m1", [M1, P])
        neg_mbias2 = sb("neg_mbias2", [P, 1])
        z_slots = sb("z_slots", [P, TILES + LAG])
        z = z_slots[:, LAG:]
        scores_out = sb("scores_out", [P, TILES])
        itemT = one_hot[0:D, 0:TILES, :].rearrange("d t p -> d (t p)")
        last_unit = hist[:, 1, 0:2 * UNIT, :].rearrange("p (k a) d -> p k (a d)", a=2)
        last_products = keys[:, :, :].rearrange("p r c -> p (r c)")[:, 0:TILES * (D + UD + ID)].rearrange("p (r c) -> p r c", r=TILES)
        weighted_two = feat[:, 1, :, :, :].rearrange("p s k (a d) -> p (s k a) d", a=2)
        signs = hist[:, 0, :, :].rearrange("p c d -> p (c d)")[:, 0:TILES * HISTORY].rearrange("p (t c) -> p t c", t=TILES)
        picked = wrapped[:, :, :]
        picked_flat = wrapped[:, :, :].rearrange("p t c -> p (t c)")

        p_lo, p_hi = bank("p_lo"), bank("p_hi")
        p_h0 = [bank("p_h0_0"), bank("p_h0_1")]
        p_h1, p_score = bank("p_h1"), bank("p_score")
        p_misc, p_misc2 = bank("p_misc"), bank("p_misc2")
        p_xT = [p_misc[:, 0:P], p_misc[:, P:2 * P]]
        p_ids = p_misc[:, 2 * P:4 * P]
        p_m0, p_m1 = p_misc2[:, 0:2 * P], p_misc2[:, 2 * P:3 * P]
        p_cd, p_z = p_misc2[CD_AT:CD_AT + CD, 3 * P:4 * P], p_misc2[:, 3 * P:3 * P + 1]

        user_ids_loaded = sem("user_ids_loaded")
        ids_loaded = sem("ids_loaded")
        history_loaded = sem("history_loaded")
        attention_weights_loaded = sem("attention_weights_loaded")
        mlp_loaded = sem("mlp_loaded")
        weights_cleared = sem("weights_cleared")
        identity_step = sem("identity_step")
        mlp_cleared = sem("mlp_cleared")
        ids_step = sem("ids_step")
        clamp_step = sem("clamp_step")
        numbers_step = sem("numbers_step")
        keys_step = sem("keys_step")
        signs_summed = sem("signs_summed")
        counts_step = sem("counts_step")
        counts_transposed = sem("counts_transposed")
        needed_ready = sem("needed_ready")
        order_step = sem("order_step")
        pick_step = sem("pick_step")
        features_picked = sem("features_picked")
        items_landed = sem("items_landed")
        users_landed = sem("users_landed")
        fold_step = sem("fold_step")
        cleared = sem("cleared")
        items_transposed = sem("items_transposed")
        itemT_copied = sem("itemT_copied")
        item_term_summed = sem("item_term_summed")
        item_term_ready = sem("item_term_ready")
        last_feat = sem("last_feat")
        last_transposed = sem("last_transposed")
        last_copied_lo = sem("last_copied_lo")
        last_copied_hi = sem("last_copied_hi")
        last_l0 = sem("last_l0")
        last_added = sem("last_added")
        last_relu0 = sem("last_relu0")
        last_l1 = sem("last_l1")
        last_relu1 = sem("last_relu1")
        last_l2 = sem("last_l2")
        last_scored = sem("last_scored")
        landed = [slot_sems(f"landed_{b}") for b in range(2)]
        index_ready = [sem(f"index_ready_{v}") for v in range(HEAD)]
        rest_index_ready = sem("rest_index_ready")
        filled = slot_sems("filled")
        rows_ready = slot_sems("rows_ready")
        sp_passed = sem("sp_passed")
        pool_passed = sem("pool_passed")
        act_passed = sem("act_passed")
        product_ready = slot_sems("product_ready")
        hist_kept = slot_sems("hist_kept")
        transposed_lo = slot_sems("transposed_lo")
        transposed_hi = slot_sems("transposed_hi")
        copied_lo = slot_sems("copied_lo")
        copied_hi = slot_sems("copied_hi")
        layer0_done = slot_sems("layer0_done")
        item_added = slot_sems("item_added")
        relu0_done = slot_sems("relu0_done")
        layer1_done = slot_sems("layer1_done")
        relu1_done = slot_sems("relu1_done")
        layer2_done = slot_sems("layer2_done")
        scored = slot_sems("scored")
        scores_reset = sem("scores_reset")
        sort_step = sem("sort_step")
        dve_passed = sem("dve_passed")
        block_sorted = sem("block_sorted")
        pool_step = sem("pool_step")
        tile_step = sem("tile_step")
        max_ready = sem("max_ready")
        exp_ready = sem("exp_ready")
        weights_ready = sem("weights_ready")
        products_ready = sem("products_ready")
        weighted_ready = sem("weighted_ready")
        history_pooled = sem("history_pooled")
        x_taken = sem("x_taken")
        diagonals_ready = sem("diagonals_ready")
        x_transposed = sem("x_transposed")
        xT_copied = sem("xT_copied")
        one_hot_ready = sem("one_hot_ready")
        cd_summed = sem("cd_summed")
        cd_copied = sem("cd_copied")
        last_x_transposed = sem("last_x_transposed")
        last_xT_copied = sem("last_xT_copied")
        m0_summed = sem("m0_summed")
        m0_ready = sem("m0_ready")
        m1_summed = sem("m1_summed")
        m1_ready = sem("m1_ready")
        m2_summed = sem("m2_summed")
        z_ready = sem("z_ready")
        sigmoid_step = sem("sigmoid_step")
        exp_z = sem("exp_z")
        unsort_step = sem("unsort_step")
        out_stored = sem("out_stored")

        block = ctx.enter_context(nc.Block())

        def blocks_of(columns):
            return (columns + (BLOCK - 1)) >> 4

        block_registers = {}

        def block_at(eng, group, n):
            eng.reg_mov(block_registers[eng], eng.snap(group * REST_GROUP + n + HEAD))
            return eng.snap(block_registers[eng], min_val=HEAD, max_val=BLOCKS - 1)

        def item_of(t):
            return x_slots[:, bass.ds(t + LAG, 1), 0:D]

        def columns_of(eng, t):
            return eng.value_load(needed[0:1, bass.ds(t, 1)], min_val=0, max_val=HISTORY)

        def own_columns_of(eng, t):
            return eng.value_load(own_most[0:1, bass.ds(t, 1)], min_val=0, max_val=HISTORY)

        TILE_PICKS = 4
        MLP_LOADS = 16 * (12 + M0 // P)
        ATTENTION_LOADS = 16 * 14

        @block.sync
        def _(sp):
            sp.dma_start(ids[:, 1, :], per_row(user_id)).then_inc(user_ids_loaded, 16)
            sp.dma_start(history[:, :, :], per_row(history_seq)).then_inc(history_loaded, 16)
            loads = [
                (wa[:, :], aW0[0:D, :]), (wb[:, :], aW0[D:2 * D, :]), (w0[D:2 * D, :], aW0[2 * D:3 * D, :]),
                (wd[:, :], aW0[3 * D:4 * D, :]),
                (b2[:, :], ab2.rearrange("(p a) -> p a", a=1).broadcast_to([P, 1])),
                (last_row[:, :], hist_W[LAST:LAST + 1, :].broadcast_to([P, D])),
            ]
            for h in range(2):
                loads += [(b0[h * A0:(h + 1) * A0, :], ab0.rearrange("(p a) -> p a", a=1)),
                          (b1[h * A1:(h + 1) * A1, :], ab1.rearrange("(p a) -> p a", a=1))]
            for h in range(2):
                loads += [(w1[h * A0:(h + 1) * A0, h * A1:(h + 1) * A1], aW1),
                          (w2[h * A1:(h + 1) * A1, h:h + 1], aW2)]
            assert 16 * len(loads) == ATTENTION_LOADS
            for n, (dst, src) in enumerate(loads):
                if n == len(loads) - 4:
                    sp.wait_ge(weights_cleared, 2)
                sp.dma_start(dst, src).then_inc(attention_weights_loaded, 16)
            sp.wait_ge(mlp_cleared, 1)
            full = cat_W.shape[0] // P
            for dst, src in (
                (cd_rows[:, 0:full, 0:C_DIM], cat_W[0:full * P, :].rearrange("(c p) n -> p c n", p=P)),
                (cd_rows[0:cat_W.shape[0] - full * P, full, 0:C_DIM], cat_W[full * P:, :]),
                (cd_rows[0:dur_W.shape[0], CAT_CHUNKS, C_DIM:CD], dur_W),
                (mw0_lo[:, :], mW0[0:P, :]), (mw0_hi[0:X_HI, :], mW0[P + CD:, :]), (mw0_hi[CD_AT:X_K, :], mW0[P:P + CD, :]),
                (mw1[:, :, :], mW1.rearrange("(c p) n -> p c n", p=P)), (mw2[:, :], mW2),
                *((mbias0[:, m:m + 1], mb0[m * P:(m + 1) * P].rearrange("(p a) -> p a", a=1)) for m in range(M0 // P)),
                (mbias1[:, :], mb1.rearrange("(p a) -> p a", a=1)),
                (mbias2[:, :], mb2.rearrange("(p a) -> p a", a=1).broadcast_to([P, 1])),
                (x_rows[:, :, D:D + UD], per_row(user_dense)),
                (x_rows[:, :, D + UD:], per_row(item_dense)),
            ):
                sp.dma_start(dst, src).then_inc(mlp_loaded, 16)

            base = sp.alloc_register("sp_blocks")
            sp.reg_mov(base, 1)
            blocks_now = sp.alloc_register("sp_blocks_now")
            landed_count = [[sp.alloc_register(f"sp_landed_{b}_{s}") for s in range(SLOTS)] for b in range(2)]
            filled_count = [sp.alloc_register(f"sp_filled_{s}") for s in range(SLOTS)]
            for register in (*landed_count[0], *landed_count[1], *filled_count):
                sp.reg_mov(register, 0)
            sp.wait_ge(attention_weights_loaded, ATTENTION_LOADS)
            sp.wait_ge(needed_ready, 1)

            def gathered(b, s, columns):
                sp.reg_add(landed_count[b][s], landed_count[b][s], 16 * columns)

            def pass_on(b, s):
                sp.wait_ge(landed[b][s], landed_count[b][s])
                sp.sem_inc(rows_ready[s], 1)

            def pass_on_block(b):
                for s in range(SLOTS):
                    gathered(b, s, UNIT)
                    pass_on(b, s)

            def fill(g, s, start):
                sp.wait_ge(hist_kept[s], g)
                sp.wait_ge(transposed_hi[s], g)
                sp.sem_inc(sp_passed, 1)
                sp.dma_start(feat[:, (HEAD - 1) & 1, s, start:UNIT, 0:D],
                             last_row[:, :].unsqueeze(1).broadcast_to([P, UNIT - start, D])).then_inc(filled[s], 16)
                sp.reg_add(filled_count[s], filled_count[s], 16)
                sp.wait_ge(filled[s], filled_count[s])
                sp.sem_inc(sp_passed, 1)

            with sp.Fori(0, TILES) as t:
                columns = own_columns_of(sp, t)
                before = sp.snap(base, min_val=1, max_val=(TILES - 1) * BLOCKS + 1)
                sp.reg_mov(blocks_now, HEAD - 1)
                for v in range(HEAD - 1):
                    pass_on_block(v & 1)

                def pass_on_columns(start):
                    s, k = divmod(start, UNIT)
                    with sp.If(columns > LEAST + start):
                        gathered(1, s, 1)
                        if k == UNIT - 1:
                            pass_on(1, s)
                        if start < BLOCK - 1:
                            pass_on_columns(start + 1)
                    with sp.Else():
                        fill(before + (HEAD - 1), s, k)
                        pass_on(1, s)
                        if s == 0:
                            fill(before + (HEAD - 1), 1, 0)
                            pass_on(1, 1)

                with sp.If(columns > LEAST):
                    gathered(1, 0, 1)
                    pass_on_columns(1)
                    sp.reg_mov(blocks_now, HEAD)
                    with sp.If(columns > REST_START):
                        with sp.Fori(HEAD, BLOCKS) as v:
                            with sp.If(columns > v * BLOCK):
                                pass_on_block(0)
                        sp.reg_mov(blocks_now, sp.snap(blocks_of(columns)))
                sp.reg_add(base, base, blocks_now)

            sp.wait_ge(unsort_step, 2)
            sp.dma_start(per_row(out), scores_out[:, :]).then_inc(out_stored, 16)
            sp.wait_ge(out_stored, 16)

        @block.gpsimd
        def _(pool):
            nc.gpsimd.memset(w1[:, :], 0.0).then_inc(weights_cleared, 1)
            nc.gpsimd.memset(w2[:, :], 0.0).then_inc(weights_cleared, 1)
            nc.gpsimd.memset(identity[:, :], 0.0).then_inc(identity_step, 1)
            pool.wait_ge(identity_step, 1)
            nc.gpsimd.affine_select(out=identity[:, :], in_=identity[:, :], compare_op=ALU.not_equal, fill=1.0,
                                    base=0, pattern=[[-1, P]], channel_multiplier=1).then_inc(identity_step, 1)
            nc.gpsimd.memset(cd_rows[:, :, :], 0.0)
            nc.gpsimd.memset(mw0_hi[:, :], 0.0).then_inc(mlp_cleared, 1)
            nc.gpsimd.iota(row_numbers_i[:, :], pattern=[[P, CAT_CHUNKS]], base=0, channel_multiplier=1).then_inc(numbers_step, 1)
            nc.gpsimd.iota(numbers_i[:, 0, :], pattern=[[-1, TILES]], base=TILES - 1, channel_multiplier=0).then_inc(numbers_step, 1)
            nc.gpsimd.iota(numbers_i[:, 1, :], pattern=[[1, TILES]], base=0, channel_multiplier=0).then_inc(numbers_step, 1)
            pool.wait_ge(ids_step, 1)
            for t in range(TILES):
                pool.indirect_dma_start(
                    x_rows[:, t, 0:D], None, user_W,
                    bass.IndirectOffsetOnAxis(ap=ids_clamped[:, 1, t:t + 1], axis=0),
                ).then_inc(users_landed, 16)
            nc.gpsimd.memset(keys_sorted[:, :, :], LAST_KEY).then_inc(cleared, 1)
            pool.wait_ge(ids_step, 2)
            for t in range(TILES):
                pool.indirect_dma_start(
                    x[:, t, 0:D], None, item_W,
                    bass.IndirectOffsetOnAxis(ap=ids_clamped[:, 0, t:t + 1], axis=0),
                ).then_inc(items_landed, 16)

            def buffers_free(s, count):
                pool.wait_ge(hist_kept[s], count)
                pool.wait_ge(transposed_hi[s], count)
                pool.sem_inc(pool_passed, 1)

            def gather(b, s, columns, index):
                for k in columns:
                    pool.indirect_dma_start(
                        feat[:, b, s, k, 0:D], None, hist_W,
                        bass.IndirectOffsetOnAxis(ap=index[:, s * UNIT + k:s * UNIT + k + 1], axis=0),
                    ).then_inc(landed[b][s], 16)

            base = pool.alloc_register("pool_blocks")
            pool.reg_mov(base, 1)
            blocks_now = pool.alloc_register("pool_blocks_now")
            rest_count = pool.alloc_register("pool_rest_count")
            pool.reg_mov(rest_count, 0)
            after_odd = pool.alloc_register("pool_after_odd")
            pool.reg_mov(after_odd, 0)
            pool.wait_ge(needed_ready, 1)
            with pool.Fori(0, TILES) as t:
                columns = own_columns_of(pool, t)
                before = pool.snap(base, min_val=1, max_val=(TILES - 1) * BLOCKS + 1)
                late = pool.snap(after_odd, min_val=0, max_val=1)
                pool.reg_mov(blocks_now, HEAD - 1)
                for v in range(HEAD - 1):
                    pool.wait_ge(index_ready[v], t + 1)
                    for s in range(SLOTS):
                        buffers_free(s, before + late if v == 0 else before + v)
                        gather(v & 1, s, range(UNIT), index_head[:, v, :])
                pool.reg_mov(after_odd, 1)
                def gather_columns(start):
                    s, k = divmod(start, UNIT)
                    if k == 0:
                        buffers_free(s, before + (HEAD - 1))
                    gather((HEAD - 1) & 1, s, [k], index_head[:, HEAD - 1, :])
                    if start < BLOCK - 1:
                        with pool.If(columns > LEAST + start + 1):
                            gather_columns(start + 1)

                with pool.If(columns > LEAST):
                    pool.reg_mov(blocks_now, HEAD)
                    pool.reg_mov(after_odd, 0)
                    pool.wait_ge(index_ready[HEAD - 1], t + 1)
                    gather_columns(0)
                    with pool.If(columns > REST_START):
                        with pool.Fori(HEAD, BLOCKS) as v:
                            with pool.If(columns > v * BLOCK):
                                pool.reg_add(rest_count, rest_count, 1)
                                pool.wait_ge(rest_index_ready, rest_count)
                                for s in range(SLOTS):
                                    buffers_free(s, before + v + 1)
                                    gather(0, s, range(UNIT), index_rest)
                        pool.reg_mov(blocks_now, pool.snap(blocks_of(columns)))
                        pool.reg_mov(after_odd, 1)
                pool.reg_add(base, base, blocks_now)

            pool.wait_ge(pick_step, TILES * TILE_PICKS + 2)
            pool.wait_ge(mlp_loaded, MLP_LOADS)
            pool.wait_ge(users_landed, 16 * TILES)
            by_feature = [P, TILES, D + UD + ID]
            nc.gpsimd.tensor_tensor(last_products, x_rows[:, :, :], row_of[:, TILES + 1, :].unsqueeze(2).broadcast_to(by_feature),
                                    ALU.mult).then_inc(products_ready, 1)
            pool.wait_ge(weights_ready, 1)
            two = slice(BLOCK, 3 * BLOCK)
            nc.gpsimd.tensor_tensor(weighted_two, hist[:, (TILES - 1) & 1, two, :],
                                    own_exp[:, two].unsqueeze(2).broadcast_to([P, 2 * BLOCK, D]), ALU.mult).then_inc(weighted_ready, 1)

        @block.scalar
        def _(act):
            for n, table_ids in ((0, item_id), (2, item_category), (3, item_dur_bkt)):
                act.dma_start(ids[:, n, :], per_row(table_ids)).then_inc(ids_loaded, 16)
            for counted in (*hist_kept, *copied_lo, *copied_hi, *relu0_done, *relu1_done, *scored,
                            x_taken, xT_copied, m0_ready, m1_ready, z_ready):
                act.sem_inc(counted, 1)
            for counted in hist_kept:
                act.sem_inc(counted, 1)
            act.wait_ge(keys_step, 5)
            for t in range(ACT_COUNTS):
                last = nc.scalar.activation(signs[:, t, :], wrapped[:, t, :], ACT.Sign, scale=-1.0, bias=sign_bias[:, :],
                                            accum_out=sign_sums[:, t:t + 1])
            last.then_inc(signs_summed, 1)
            act.wait_ge(attention_weights_loaded, ATTENTION_LOADS)
            act.wait_ge(items_transposed, 2)
            nc.scalar.activation(itemT[:, N:2 * N], p_hi[0:D, :], ACT.Copy).then_inc(itemT_copied, 1)
            for c in range(2):
                act.wait_ge(item_term_summed, c + 1)
                nc.scalar.activation(item_term[:, c * N:(c + 1) * N], p_h0[c][:, :], ACT.Identity,
                                     bias=b0[:, :]).then_inc(item_term_ready, 1)
            act.wait_ge(last_transposed, 2)
            nc.scalar.activation(featT[:, 1, N:2 * N], p_hi[:, :], ACT.Copy).then_inc(last_copied_hi, 1)
            act.wait_ge(last_added, 2)
            nc.scalar.activation(h0[:, 1, :], h0[:, 1, :], ACT.Relu).then_inc(last_relu0, 1)
            act.wait_ge(last_l1, 1)
            nc.scalar.activation(h1[:, 1, :], p_h1[0:2 * A1, :], ACT.Relu, bias=b1[:, :]).then_inc(last_relu1, 1)

            act.wait_ge(mlp_loaded, MLP_LOADS)
            nc.scalar.activation(neg_mbias2[:, :], mbias2[:, :], ACT.Copy, scale=-1.0).then_inc(sigmoid_step, 1)
            act.wait_ge(users_landed, 16 * TILES)
            act.wait_ge(items_landed, 16 * TILES)
            act.wait_ge(needed_ready, 1)
            block_registers[act] = act.alloc_register("act_block")
            base = act.alloc_register("act_blocks")
            act.reg_mov(base, 1)
            late_at = act.alloc_register("act_late_scores")
            act.reg_mov(late_at, 2 * COLS)

            def relu1(s, g):
                act.wait_ge(layer2_done[s], g)
                act.wait_ge(layer1_done[s], g + 1)
                nc.scalar.activation(h1[:, s, :], p_h1[0:2 * A1, :], ACT.Relu, bias=b1[:, :]).then_inc(relu1_done[s], 1)

            def put_scores(s, g, at):
                act.wait_ge(layer2_done[s], g + 1)
                nc.scalar.activation(scores[:, bass.ds(at, UNIT)], p_score[:, s * UNIT:(s + 1) * UNIT], ACT.Identity,
                                     bias=b2[:, :]).then_inc(scored[s], 1)

            def exponentials(t):
                act.wait_ge(max_ready, t + 1)
                nc.scalar.activation(expd[:, :], tile_scores[:, :], ACT.Exp,
                                     bias=neg_max[:, :], accum_out=exp_sum[:, :]).then_inc(exp_ready, 1)

            def act_unit(t, v, g, s, b, between=lambda: None):
                act.wait_ge(rows_ready[s], g)
                nc.scalar.activation(
                    hist[:, bass.ds(t & 1, 1), bass.ds(v * BLOCK + s * UNIT, UNIT), :].rearrange("p a c d -> p (a c) d"),
                    feat[:, b, s, :, 0:D], ACT.Copy).then_inc(hist_kept[s], 1)
                act.wait_ge(transposed_lo[s], g + 1)
                nc.scalar.activation(featT[:, s, 0:N], p_lo[:, :], ACT.Copy).then_inc(copied_lo[s], 1)
                act.wait_ge(transposed_hi[s], g + 2)
                nc.scalar.activation(featT[:, s, N:2 * N], p_hi[:, :], ACT.Copy).then_inc(copied_hi[s], 1)
                relu1(1 - s, g)
                between()
                act.wait_ge(item_added[s], g + 1)
                nc.scalar.activation(h0[:, s, :], h0[:, s, :], ACT.Relu).then_inc(relu0_done[s], 1)
                if s == 0:
                    put_scores(1, g, act.snap(late_at, min_val=0, max_val=SCORE_COLS - UNIT))
                else:
                    put_scores(0, g, (t & 1) * COLS + v * BLOCK)
                    act.reg_mov(late_at, act.snap((t & 1) * COLS + v * BLOCK + UNIT))

            def take_x(t):
                if isinstance(t, int) and t == TILES:
                    act.wait_ge(history_pooled, t + 1)
                act.wait_ge(x_transposed, t + 1)
                nc.scalar.activation(x_now[:, D:2 * D].unsqueeze(1), x_slots[:, bass.ds(t, 1), 0:D], ACT.Copy)
                if isinstance(t, int) and t > TILES:
                    nc.scalar.activation(x_now[:, X_DIM:], x_slots[:, t, 2 * D:], ACT.Copy).then_inc(x_taken, 1)
                else:
                    nc.scalar.activation(x_now[:, X_POOL:].unsqueeze(1), x_slots[:, bass.ds(t, 1), D:], ACT.Copy).then_inc(x_taken, 1)
                act.wait_ge(x_taken, t + 2)
                act.sem_inc(act_passed, 1)
                for n in range(2):
                    ins = nc.scalar.activation(ids_diagonal[:, n, :], identity[:, :], ACT.Copy,
                                               scale=x_now[:, X_IDS + n:X_IDS + n + 1])
                ins.then_inc(diagonals_ready, 1)

            def copy_xT(t):
                act.wait_ge(m0_summed, t + 1)
                act.wait_ge(x_transposed, t + 2)
                if isinstance(t, int) and t > TILES:
                    act.wait_ge(one_hot_ready, t + 2)
                last = nc.scalar.activation(xT_lo[:, :], p_xT[0], ACT.Copy)
                if not (isinstance(t, int) and t > TILES):
                    last = nc.scalar.activation(xT_hi[0:X_HI, :], p_xT[1][0:X_HI, :], ACT.Copy)
                last.then_inc(xT_copied, 1)

            def copy_cd(t):
                act.wait_ge(cd_summed, t + 2)
                nc.scalar.activation(xT_hi[CD_AT:X_K, :], p_cd, ACT.Copy).then_inc(cd_copied, 1)

            def copy_last_xT():
                act.wait_ge(last_x_transposed, 1)
                nc.scalar.activation(xT_hi[0:X_HI, :], p_xT[1][0:X_HI, :], ACT.Copy).then_inc(last_xT_copied, 1)

            def relu_m0(t):
                act.wait_ge(m1_summed, t + 1)
                act.wait_ge(m0_summed, t + 2)
                for m in range(M0 // P):
                    ins = nc.scalar.activation(m0[:, m, :], p_m0[:, m * P:(m + 1) * P], ACT.Relu, bias=mbias0[:, m:m + 1])
                ins.then_inc(m0_ready, 1)

            def relu_m1(t):
                act.wait_ge(m2_summed, t + 1)
                act.wait_ge(m1_summed, t + 2)
                nc.scalar.activation(m1[:, :], p_m1, ACT.Relu, bias=mbias1[:, :]).then_inc(m1_ready, 1)

            def put_z(t):
                act.wait_ge(m2_summed, t + 2)
                nc.scalar.activation(z_slots[:, bass.ds(t, 1)], p_z, ACT.Copy).then_inc(z_ready, 1)

            mlp_steps = {(0, 0): take_x, (0, 1): copy_xT, (1, 0): copy_cd, (1, 1): relu_m0, (2, 0): relu_m1, (2, 1): put_z}

            with act.Fori(0, TILES) as t:
                columns = columns_of(act, t + 1)
                before = act.snap(base, min_val=1, max_val=TILES * BLOCKS + 1)
                act.wait_ge(history_pooled, t + 1)
                act.sem_inc(act_passed, 1)
                act.wait_ge(scores_reset, t + 1)
                act.sem_inc(act_passed, 1)
                for v in range(HEAD - 1):
                    for s in range(SLOTS):
                        act_unit(t, v, before + v, s, v & 1, (lambda: exponentials(t)) if (v, s) == (0, 1) else (lambda: None))
                        if (v, s) in mlp_steps:
                            mlp_steps[v, s](t)
                with act.If(columns > LEAST):
                    for s in range(SLOTS):
                        act_unit(t, HEAD - 1, before + (HEAD - 1), s, (HEAD - 1) & 1)
                    with act.If(columns > REST_START):
                        with act.Fori(0, REST_GROUPS) as group:
                            with act.If(columns > group * (REST_GROUP * BLOCK) + REST_START):
                                with act.Fori(0, REST_GROUP) as n:
                                    with act.If(columns > (group * REST_GROUP + n) * BLOCK + REST_START):
                                        v = block_at(act, group, n)
                                        for s in range(SLOTS):
                                            act_unit(t, v, before + v, s, 0)
                act.reg_add(base, base, act.snap(blocks_of(columns)))
            g = act.snap(base, min_val=1, max_val=TILES * BLOCKS + 1)
            relu1(1, g)
            take_x(TILES)
            put_scores(1, g, act.snap(late_at, min_val=0, max_val=SCORE_COLS - UNIT))
            copy_xT(TILES)
            exponentials(TILES)
            take_x(TILES + 1)
            copy_cd(TILES)
            relu_m0(TILES)
            relu_m1(TILES)
            put_z(TILES)
            copy_xT(TILES + 1)
            copy_cd(TILES + 1)
            copy_last_xT()
            relu_m0(TILES + 1)
            relu_m1(TILES + 1)
            put_z(TILES + 1)
            act.wait_ge(sigmoid_step, 1)
            act.wait_ge(z_ready, TILES + LAG + 1)
            nc.scalar.activation(z, z, ACT.Exp, scale=-1.0, bias=neg_mbias2[:, :]).then_inc(exp_z, 1)

        @block.tensor
        def _(pe):
            for counted in (*transposed_lo, *transposed_hi, *layer0_done, *layer1_done, *layer2_done,
                            x_transposed, cd_summed, m0_summed, m1_summed, m2_summed):
                pe.sem_inc(counted, 1)
            for counted in transposed_hi:
                pe.sem_inc(counted, 1)
            pe.wait_ge(identity_step, 2)
            pe.wait_ge(order_step, 8)
            nc.tensor.transpose(p_misc[0:TILES, 0:P], counts_picked[:, :], identity[:, :]).then_inc(counts_transposed, 1)
            pe.wait_ge(counts_step, 3)
            nc.tensor.matmul(p_misc2[0:1, 0:TILES], counts_max[:, :], identity[0:TILES, 0:TILES],
                             start=True, stop=True).then_inc(counts_transposed, 1)
            pe.wait_ge(items_landed, 16 * TILES)
            for c, dst in enumerate((p_lo, p_hi)):
                for k in range(HALF):
                    last = nc.tensor.transpose(dst[0:D, k * P:(k + 1) * P], x[:, c * HALF + k, 0:D], identity[:, :])
                last.then_inc(items_transposed, 1)
            pe.wait_ge(fold_step, 3)
            pe.wait_ge(itemT_copied, 2)
            for c in range(2):
                nc.tensor.matmul(p_h0[c][:, :], w_item[:, :], itemT[:, c * N:(c + 1) * N],
                                 start=True, stop=True).then_inc(item_term_summed, 1)
            pe.wait_ge(last_feat, 2)
            for c, dst in enumerate((p_lo, p_hi)):
                for k in range(HALF):
                    last = nc.tensor.transpose(dst[:, k * P:(k + 1) * P], last_unit[:, c * HALF + k, :], identity[:, :])
                last.then_inc(last_transposed, 1)
            pe.wait_ge(last_copied_lo, 1)
            pe.wait_ge(item_term_ready, 2)
            nc.tensor.matmul(p_h0[1][0:A0, :], w0[:, :], featT[:, 1, 0:N], start=True, stop=True)
            pe.wait_ge(last_copied_hi, 1)
            nc.tensor.matmul(p_h0[1][A0:2 * A0, :], w0[:, :], featT[:, 1, N:2 * N],
                             start=True, stop=True).then_inc(last_l0, 1)
            pe.wait_ge(last_relu0, 1)
            nc.tensor.matmul(p_h1[0:2 * A1, :], w1[:, :], h0[:, 1, :], start=True, stop=True).then_inc(last_l1, 1)
            pe.wait_ge(last_relu1, 1)
            for k in range(HALF):
                last = nc.tensor.matmul(p_score[:, k:UNIT:HALF], h1[:, 1, k * P:(k + 1) * P], w2[:, :],
                                        start=True, stop=True)
            last.then_inc(last_l2, 1)
            pe.wait_ge(last_scored, 1)

            pe.wait_ge(mlp_loaded, MLP_LOADS)
            pe.wait_ge(needed_ready, 1)
            block_registers[pe] = pe.alloc_register("pe_block")
            base = pe.alloc_register("pe_blocks")
            pe.reg_mov(base, 1)
            def layer1(s, g):
                pe.wait_ge(relu1_done[1 - s], g if s == 1 else g + 1)
                pe.wait_ge(relu0_done[s], g if s == 1 else g + 1)
                nc.tensor.matmul(p_h1[0:2 * A1, :], w1[:, :], h0[:, s, :], start=True, stop=True).then_inc(layer1_done[s], 1)

            def layer2(s, g):
                pe.wait_ge(scored[s], g)
                pe.wait_ge(relu1_done[s], g + 1)
                for k in range(HALF):
                    last = nc.tensor.matmul(p_score[:, s * UNIT + k:(s + 1) * UNIT:HALF],
                                            h1[:, s, k * P:(k + 1) * P], w2[:, :], start=True, stop=True)
                last.then_inc(layer2_done[s], 1)

            def pe_unit(g, s, b):
                pe.wait_ge(product_ready[s], g + 1)
                pe.wait_ge(copied_lo[1 - s], g + s)
                for k in range(HALF):
                    last = nc.tensor.transpose(p_lo[:, k * P:(k + 1) * P], feat[:, b, s, k, :], identity[:, :])
                last.then_inc(transposed_lo[s], 1)
                pe.wait_ge(copied_hi[1 - s], g + s)
                for k in range(HALF):
                    last = nc.tensor.transpose(p_hi[:, k * P:(k + 1) * P], feat[:, b, s, HALF + k, :], identity[:, :])
                last.then_inc(transposed_hi[s], 1)
                layer1(1 - s, g)
                pe.wait_ge(item_added[s], g)
                pe.wait_ge(copied_lo[s], g + 1)
                nc.tensor.matmul(p_h0[s][0:A0, :], w0[:, :], featT[:, s, 0:N], start=True, stop=True)
                pe.wait_ge(copied_hi[s], g + 1)
                nc.tensor.matmul(p_h0[s][A0:2 * A0, :], w0[:, :], featT[:, s, N:2 * N],
                                 start=True, stop=True).then_inc(layer0_done[s], 1)
                layer2(1 - s, g)

            def transpose_x(t):
                pe.wait_ge(one_hot_ready, t + 1)
                pe.wait_ge(xT_copied, t + 1)
                pe.wait_ge(features_picked, t + 1)
                pe.wait_ge(diagonals_ready, t + 1)
                nc.tensor.transpose(p_xT[0], x_now[:, 0:P], identity[:, :])
                if not (isinstance(t, int) and t > TILES):
                    nc.tensor.transpose(p_xT[1][0:X_HI, :], x_now[:, P:X_DIM], identity[:, :])
                for n in range(2):
                    last = nc.tensor.matmul(p_ids[:, n * P:(n + 1) * P], ones[:, :], ids_diagonal[:, n, :],
                                            start=True, stop=True)
                last.then_inc(x_transposed, 1)

            def sum_cd(t):
                pe.wait_ge(z_ready, t + 1)
                pe.wait_ge(one_hot_ready, t + 2)
                for c in range(CHUNKS):
                    last = nc.tensor.matmul(p_cd, cd_rows[:, c, :], one_hot[:, c, :], start=(c == 0), stop=(c == CHUNKS - 1))
                last.then_inc(cd_summed, 1)

            def transpose_last_x():
                pe.wait_ge(xT_copied, TILES + LAG + 1)
                pe.wait_ge(history_pooled, TILES + LAG)
                nc.tensor.transpose(p_xT[1][0:X_HI, :], x_now[:, P:X_DIM], identity[:, :]).then_inc(last_x_transposed, 1)
                pe.wait_ge(last_xT_copied, 1)

            def sum_m0(t):
                pe.wait_ge(m0_ready, t + 1)
                pe.wait_ge(xT_copied, t + 2)
                pe.wait_ge(cd_copied, t + 1)
                for m in range(M0 // P):
                    nc.tensor.matmul(p_m0[:, m * P:(m + 1) * P], mw0_lo[:, m * P:(m + 1) * P], xT_lo[:, :],
                                     start=True, stop=False)
                    last = nc.tensor.matmul(p_m0[:, m * P:(m + 1) * P], mw0_hi[:, m * P:(m + 1) * P], xT_hi[:, :],
                                            start=False, stop=True)
                last.then_inc(m0_summed, 1)

            def sum_m1(t):
                pe.wait_ge(m1_ready, t + 1)
                pe.wait_ge(m0_ready, t + 2)
                for m in range(M0 // P):
                    last = nc.tensor.matmul(p_m1, mw1[:, m, :], m0[:, m, :], start=(m == 0), stop=(m == M0 // P - 1))
                last.then_inc(m1_summed, 1)

            def sum_m2(t):
                pe.wait_ge(m1_ready, t + 2)
                nc.tensor.matmul(p_z, m1[:, :], mw2[:, :], start=True, stop=True).then_inc(m2_summed, 1)

            mlp_steps = {(0, 1): transpose_x, (1, 0): sum_cd, (1, 1): sum_m0, (2, 0): sum_m1, (2, 1): sum_m2}

            with pe.Fori(0, TILES) as t:
                columns = columns_of(pe, t + 1)
                before = pe.snap(base, min_val=1, max_val=TILES * BLOCKS + 1)
                for v in range(HEAD - 1):
                    for s in range(SLOTS):
                        pe_unit(before + v, s, v & 1)
                        if (v, s) in mlp_steps:
                            mlp_steps[v, s](t)
                with pe.If(columns > LEAST):
                    for s in range(SLOTS):
                        pe_unit(before + (HEAD - 1), s, (HEAD - 1) & 1)
                    with pe.If(columns > REST_START):
                        with pe.Fori(0, REST_GROUPS) as group:
                            with pe.If(columns > group * (REST_GROUP * BLOCK) + REST_START):
                                with pe.Fori(0, REST_GROUP) as n:
                                    with pe.If(columns > (group * REST_GROUP + n) * BLOCK + REST_START):
                                        for s in range(SLOTS):
                                            pe_unit(before + block_at(pe, group, n), s, 0)
                pe.reg_add(base, base, pe.snap(blocks_of(columns)))
            g = pe.snap(base, min_val=1, max_val=TILES * BLOCKS + 1)
            layer1(1, g)
            layer2(1, g)
            for position in sorted(mlp_steps):
                mlp_steps[position](TILES)
                if mlp_steps[position] == sum_m0:
                    transpose_x(TILES + 1)
            sum_cd(TILES + 1)
            transpose_last_x()
            sum_m0(TILES + 1)
            sum_m1(TILES + 1)
            sum_m2(TILES + 1)

        @block.vector
        def _(dve):
            for counted in (*product_ready, *item_added, block_sorted, history_pooled):
                dve.sem_inc(counted, 1)
            dve.sem_inc(sort_step, 4)
            dve.sem_inc(one_hot_ready, 1)
            dve.sem_inc(pool_step, 3)
            nc.vector.memset(sign_bias[:, :], LAST - 0.5).then_inc(cleared, 1)
            for never_written, value in ((ones, 1.0), (masked, MASKED), (own_exp, 0.0), (pooled, 0.0), (scores, 0.0),
                                         (xT_hi, 0.0)):
                nc.vector.memset(never_written[:, :], value).then_inc(cleared, 1)
            nc.vector.memset(x_slots[:, 0:LAG, :], 0.0).then_inc(cleared, 1)
            nc.vector.memset(row_of[:, :, :], 0.0).then_inc(cleared, 1)
            def clamp_ids(tables, step):
                for n, table in tables:
                    last = nc.vector.tensor_scalar(ids_f[:, n, :], ids[:, n, :], 0.0, float(table.shape[0]), ALU.is_lt, ALU.mult)
                last.then_inc(clamp_step, 1)
                dve.wait_ge(clamp_step, step + 1)
                for n, table in tables:
                    last = nc.vector.tensor_tensor(ids_f[:, n, :], ids_f[:, n, :], ids[:, n, :], ALU.add)
                last.then_inc(clamp_step, 1)
                dve.wait_ge(clamp_step, step + 2)
                for n, table in tables:
                    last = nc.vector.tensor_scalar(ids_clamped[:, 1, :] if n == 1 else ids_f[:, n, :], ids_f[:, n, :], 0.0,
                                                   float(table.shape[0] - 1), ALU.max, ALU.min)
                return last

            dve.wait_ge(user_ids_loaded, 16)
            clamp_ids([(1, user_W)], 0).then_inc(ids_step, 1)
            nc.vector.memset(needed[:, 0:TILES + 1], 0)
            nc.vector.memset(needed[:, TILES + 1:TILES + 3], LEAST).then_inc(keys_step, 2)
            dve.wait_ge(numbers_step, 3)
            nc.vector.tensor_copy(row_numbers[:, :], row_numbers_i[:, :])
            nc.vector.tensor_copy(numbers[:, :, :], numbers_i[:, :, :]).then_inc(order_step, 1)
            dve.wait_ge(history_loaded, 16)
            nc.vector.tensor_scalar(wrapped[:, :, :], history[:, :, :], 0.0, float(LAST + 1), ALU.is_lt,
                                    ALU.mult).then_inc(keys_step, 1)
            dve.wait_ge(keys_step, 3)
            nc.vector.tensor_tensor(wrapped[:, :, :], wrapped[:, :, :], history[:, :, :], ALU.add).then_inc(keys_step, 1)
            dve.wait_ge(keys_step, 4)
            nc.vector.tensor_scalar(wrapped[:, :, :], wrapped[:, :, :], 0.0, float(LAST), ALU.max,
                                    ALU.min).then_inc(keys_step, 1)
            dve.wait_ge(keys_step, 5)
            for t in range(ACT_COUNTS, TILES):
                last = nc.vector.tensor_scalar(signs[:, t, :], wrapped[:, t, :], float(LAST), 0.0, ALU.is_lt, ALU.add,
                                               accum_out=counts[:, t:t + 1])
            last.then_inc(counts_step, 1)
            dve.wait_ge(ids_loaded, 16 * 3)
            clamp_ids([(0, item_W), (2, cat_W), (3, dur_W)], 2).then_inc(order_step, 1)
            dve.wait_ge(signs_summed, 1)
            nc.vector.tensor_scalar(counts[:, 0:ACT_COUNTS], sign_sums[:, :], 0.5, 0.5 * HISTORY, ALU.mult, ALU.add).then_inc(counts_step, 1)
            dve.wait_ge(order_step, 2)
            dve.wait_ge(counts_step, 2)
            nc.vector.scalar_tensor_tensor(out=rank_by[:, :], in0=counts[:, :], scalar=float(TILES), in1=numbers[:, 0, :],
                                           op0=ALU.mult, op1=ALU.add).then_inc(order_step, 1)
            dve.wait_ge(order_step, 3)
            by_row = [P, TILES, TILES]
            nc.vector.tensor_tensor(beats[:, :, :], rank_by[:, :].unsqueeze(1).broadcast_to(by_row),
                                    rank_by[:, :].unsqueeze(2).broadcast_to(by_row), ALU.is_gt).then_inc(order_step, 1)
            dve.wait_ge(order_step, 4)
            nc.vector.tensor_reduce(rank[:, :], beats[:, :, :], op=ALU.add, axis=AX.X).then_inc(order_step, 1)
            dve.wait_ge(order_step, 5)
            dve.wait_ge(cleared, 9)
            nc.vector.tensor_tensor(row_of[:, LAG:LAG + TILES, :], rank[:, :].unsqueeze(1).broadcast_to(by_row),
                                    numbers[:, 1, :].unsqueeze(2).broadcast_to(by_row), ALU.is_equal).then_inc(order_step, 1)
            dve.wait_ge(order_step, 6)
            tile_rows = row_of[:, LAG:LAG + TILES, :]
            before_keys = keys[:, :, :].rearrange("p r c -> p (r c)")
            id_products = before_keys[:, 0:4 * TILES * TILES].rearrange("p (n t r) -> p n t r", n=4, t=TILES)
            count_products = before_keys[:, 4 * TILES * TILES:5 * TILES * TILES].rearrange("p (t r) -> p t r", t=TILES)
            nc.vector.tensor_tensor(id_products, ids_f[:, :, :].unsqueeze(2).broadcast_to([P, 4, TILES, TILES]),
                                    tile_rows.unsqueeze(1).broadcast_to([P, 4, TILES, TILES]), ALU.mult)
            nc.vector.tensor_tensor(count_products, counts[:, :].unsqueeze(1).broadcast_to(by_row), tile_rows,
                                    ALU.mult).then_inc(order_step, 1)
            dve.wait_ge(order_step, 7)
            nc.vector.tensor_reduce(ids_picked[:, :, :], id_products, op=ALU.add, axis=AX.X)
            nc.vector.tensor_reduce(counts_picked[:, :], count_products, op=ALU.add, axis=AX.X).then_inc(order_step, 1)
            dve.wait_ge(order_step, 8)
            nc.vector.tensor_copy(ids_clamped[:, 0, :], ids_picked[:, 0, :]).then_inc(ids_step, 1)
            for n in range(2):
                nc.vector.tensor_copy(x[:, :, 2 * D + n], ids_picked[:, 2 + n, :])
            nc.vector.scalar_tensor_tensor(out=keys[:, 0:TILES, :], in0=history[:, :, :], scalar=0.0,
                                           in1=wrapped[:, :, :], op0=ALU.is_equal, op1=ALU.subtract).then_inc(keys_step, 1)
            dve.wait_ge(keys_step, 6)

            def pick_keys(t):
                return nc.vector.tensor_tensor(picked, keys[:, :, :],
                                               row_of[:, bass.ds(t + LAG, 1), :].rearrange("p a r -> p (a r)").unsqueeze(2)
                                               .broadcast_to([P, TILES, HISTORY]), ALU.mult)

            def sum_keys(destination):
                return nc.vector.tensor_reduce(destination, picked.rearrange("p r c -> p c r"), op=ALU.add, axis=AX.X)

            def load_keys():
                return nc.vector.tensor_copy(unsorted[:, :], keys_next[:, :])

            def sum_features(products, t):
                for destination, source in ((x_now[:, 0:D], products[:, :, 0:D]), (x_now[:, X_UD:X_POOL], products[:, :, D:])):
                    last = nc.vector.tensor_reduce(destination, source.rearrange("p r c -> p c r"), op=ALU.add, axis=AX.X)
                last.then_inc(features_picked, 1)
                dve.wait_ge(features_picked, t + 1)

            def pick_features(t, picks):
                dve.wait_ge(x_transposed, t + 1)
                dve.wait_ge(pick_step, picks)
                dve.sem_inc(dve_passed, 1)
                products = picked_flat[:, 0:TILES * (D + UD + ID)].rearrange("p (r c) -> p r c", r=TILES)
                nc.vector.tensor_tensor(products, x_rows[:, :, :],
                                        row_of[:, bass.ds(t, 1), :].rearrange("p a r -> p (a r)").unsqueeze(2)
                                        .broadcast_to([P, TILES, D + UD + ID]), ALU.mult).then_inc(pick_step, 1)
                dve.wait_ge(pick_step, picks + 1)
                sum_features(products, t)
                dve.sem_inc(pick_step, 1)

            found = top[:, :, :].rearrange("p s c -> p (s c)")

            def sort_block(t, v, sorted_before):
                dve.wait_ge(block_sorted, sorted_before)
                for s in range(SLOTS):
                    dve.wait_ge(sort_step, sorted_before * 4 + 2 * s)
                    dve.sem_inc(dve_passed, 1)
                    nc.vector.max(out=top[:, s, :], in_=unsorted[:, :]).then_inc(sort_step, 1)
                    dve.wait_ge(sort_step, sorted_before * 4 + 2 * s + 1)
                    dve.sem_inc(dve_passed, 1)
                    nc.vector.match_replace(out=unsorted[:, :], in_to_replace=top[:, s, :], in_values=unsorted[:, :],
                                            imm_value=LAST_KEY).then_inc(sort_step, 1)
                nc.vector.tensor_copy(keys_sorted[:, bass.ds(t + 1, 1), bass.ds(v * BLOCK, BLOCK)], found.unsqueeze(1))

            def index_block(destination):
                nc.vector.tensor_scalar(destination, found, -1.0, 0.0, ALU.mult, ALU.max).then_inc(block_sorted, 1)

            def index_head_block(v, sorted_before):
                index_block(index_head[:, v, :])
                dve.wait_ge(block_sorted, sorted_before + 1)
                dve.sem_inc(index_ready[v], 1)

            def index_rest_block(t, v):
                index_block(index_rest_sorted[:, bass.ds(t & 1, 1), bass.ds((v - HEAD) * BLOCK, BLOCK)]
                            .rearrange("p a c -> p (a c)"))

            def pool_block(t, v, pooled_before):
                columns = bass.ds(v * BLOCK, BLOCK)
                for s in range(SLOTS):
                    dve.wait_ge(hist_kept[s], pooled_before + 2)
                nc.vector.tensor_tensor(
                    weighted[:, :, :], hist[:, bass.ds(t & 1, 1), columns, :].rearrange("p a c d -> p (a c) d"),
                    own_exp[:, columns].unsqueeze(2).broadcast_to([P, BLOCK, D]), ALU.mult).then_inc(pool_step, 1)
                dve.wait_ge(pool_step, pooled_before * 3 + 1)
                nc.vector.tensor_reduce(part[:, :], weighted[:, :, :].rearrange("p c d -> p d c"), op=ALU.add,
                                        axis=AX.X).then_inc(pool_step, 1)
                dve.wait_ge(pool_step, pooled_before * 3 + 2)
                nc.vector.tensor_tensor(pooled[:, :], pooled[:, :], part[:, :], ALU.add).then_inc(pool_step, 1)
                dve.wait_ge(pool_step, pooled_before * 3 + 3)
                dve.sem_inc(dve_passed, 1)

            pick_keys(0).then_inc(keys_step, 1)
            dve.wait_ge(keys_step, 7)
            sum_keys(unsorted[:, :]).then_inc(keys_step, 1)
            dve.wait_ge(keys_step, 8)
            dve.wait_ge(cleared, 10)
            sort_block(0, 0, 1)
            index_head_block(0, 1)

            dve.wait_ge(counts_transposed, 1)
            nc.vector.reduce_max(counts_max[:, :], p_misc[0:TILES, 0:P], AX.X).then_inc(counts_step, 1)
            dve.wait_ge(counts_transposed, 2)
            nc.vector.tensor_copy(own_most[:, :], p_misc2[0:1, 0:TILES])
            nc.vector.tensor_scalar(needed[:, 1:TILES + 1], p_misc2[0:1, 0:TILES], float(LEAST), None, ALU.max).then_inc(needed_ready, 1)
            dve.wait_ge(needed_ready, 1)
            nc.vector.tensor_tensor(needed_most[:, :], needed[:, 0:TILES + 1], needed[:, 1:TILES + 2], ALU.max).then_inc(counts_step, 1)
            dve.wait_ge(counts_step, 4)
            nc.vector.tensor_tensor(needed_most[:, :], needed_most[:, :], needed[:, 2:TILES + 3], ALU.max).then_inc(counts_step, 1)
            dve.wait_ge(counts_step, 5)

            dve.wait_ge(attention_weights_loaded, ATTENTION_LOADS)
            nc.vector.tensor_tensor(w0[0:D, :], wa[:, :], wd[:, :], ALU.add).then_inc(fold_step, 1)
            for h in range(2):
                nc.vector.tensor_tensor(w_item[:, h * A0:(h + 1) * A0], wb[:, :], wd[:, :],
                                        ALU.subtract).then_inc(fold_step, 1)
            dve.wait_ge(items_transposed, 1)
            nc.vector.tensor_copy(itemT[:, 0:N], p_lo[0:D, :]).then_inc(itemT_copied, 1)
            last_rows = last_row[:, :].unsqueeze(1).broadcast_to([P, TILES, D])
            nc.vector.tensor_copy(last_unit[:, :, 0:D], last_rows).then_inc(last_feat, 1)
            dve.wait_ge(items_landed, 16 * TILES)
            nc.vector.tensor_tensor(last_unit[:, :, D:2 * D], last_rows, x[:, :, 0:D], ALU.mult).then_inc(last_feat, 1)
            sort_block(0, 1, 2)
            index_head_block(1, 2)
            dve.wait_ge(last_transposed, 1)
            nc.vector.tensor_copy(featT[:, 1, 0:N], p_lo[:, :]).then_inc(last_copied_lo, 1)
            sort_block(0, 2, 3)
            index_head_block(2, 3)
            dve.wait_ge(last_l0, 1)
            for h in range(2):
                part_rows = slice(h * A0, (h + 1) * A0)
                nc.vector.tensor_tensor(h0[part_rows, 1, :], p_h0[1][part_rows, :], item_term[part_rows, h * N:(h + 1) * N],
                                        ALU.add).then_inc(last_added, 1)
            pick_keys(1).then_inc(pick_step, 1)
            dve.wait_ge(pick_step, 1)
            sum_keys(keys_next[:, :]).then_inc(pick_step, 1)
            columns0 = columns_of(dve, 1)
            with dve.If(columns0 > LEAST):
                sort_block(0, HEAD - 1, HEAD)
                index_head_block(HEAD - 1, HEAD)
                with dve.If(columns0 > REST_START):
                    with dve.Fori(HEAD, BLOCKS) as v:
                        with dve.If(columns0 > v * BLOCK):
                            sort_block(0, v, v + 1)
                            index_rest_block(0, v)
            dve.wait_ge(last_l2, 1)
            nc.vector.tensor_scalar(last_score[:, :], p_score[:, 0:TILES], b2[:, :], None, ALU.add).then_inc(last_scored, 1)
            dve.wait_ge(last_scored, 1)

            block_registers[dve] = dve.alloc_register("dve_block")
            base = dve.alloc_register("dve_blocks")
            dve.reg_mov(base, 1)
            pooled_base = dve.alloc_register("dve_blocks_pooled")
            dve.reg_mov(pooled_base, 1)
            rest_count = dve.alloc_register("dve_rest_count")
            dve.reg_mov(rest_count, 0)
            TILE_STEPS = 8

            def softmax(t, steps_before, meanwhile=lambda: None):
                tile_keys = keys_sorted[:, bass.ds(t, 1), 0:HISTORY]
                nc.vector.tensor_copy(tile_scores[:, :], scores[:, bass.ds(((t + 1) & 1) * COLS, HISTORY)]).then_inc(tile_step, 1)
                nc.vector.tensor_scalar(padding[:, :].unsqueeze(1), tile_keys, 0.5, None, ALU.is_gt).then_inc(tile_step, 1)
                dve.wait_ge(tile_step, steps_before + 3)
                dve.sem_inc(dve_passed, 1)
                nc.vector.copy_predicated(tile_scores[:, :], padding[:, :], masked[:, :]).then_inc(tile_step, 1)
                dve.wait_ge(tile_step, steps_before + 4)
                nc.vector.tensor_reduce(neg_max[:, :], tile_scores[:, :], op=ALU.max, axis=AX.X, negate=True).then_inc(max_ready, 1)
                meanwhile()
                dve.wait_ge(exp_ready, t + 1)
                nc.vector.reciprocal(inv_sum[:, :], exp_sum[:, :]).then_inc(tile_step, 1)
                nc.vector.scalar_tensor_tensor(out=last_exp[:, :].unsqueeze(1), in0=tile_keys, scalar=LAST_KEY,
                                               in1=expd[:, :].unsqueeze(1), op0=ALU.is_le, op1=ALU.mult,
                                               accum_out=last_exp_sum[:, :]).then_inc(tile_step, 1)
                dve.wait_ge(tile_step, steps_before + 6)
                nc.vector.tensor_tensor(own_exp[:, 0:HISTORY], expd[:, :], last_exp[:, :], ALU.subtract).then_inc(tile_step, 1)
                nc.vector.tensor_scalar(pooled[:, :], last_row[:, :], last_exp_sum[:, :], None, ALU.mult).then_inc(tile_step, 1)
                dve.wait_ge(tile_step, steps_before + 8)
                dve.sem_inc(dve_passed, 1)

            def finish_pooling(t):
                nc.vector.tensor_scalar(x_slots[:, bass.ds(t, 1), D:2 * D], pooled[:, :].unsqueeze(1),
                                        inv_sum[:, :], None, ALU.mult).then_inc(history_pooled, 1)

            def dve_unit(t, g, s, b, between):
                dve.wait_ge(rows_ready[s], g)
                nc.vector.tensor_tensor(feat[:, b, s, :, D:2 * D], feat[:, b, s, :, 0:D],
                                        item_of(t).broadcast_to([P, UNIT, D]), ALU.mult).then_inc(product_ready[s], 1)
                between()
                dve.wait_ge(layer1_done[s], g + s)
                dve.wait_ge(layer0_done[s], g + 1)
                nc.vector.tensor_tensor(
                    h0[:, s, :].rearrange("p (k b) -> p k b", k=HALF), p_h0[s][:, :].rearrange("p (k b) -> p k b", k=HALF),
                    item_term[:, bass.ds(t * P, P)].unsqueeze(1).broadcast_to([P, HALF, P]),
                    ALU.add).then_inc(item_added[s], 1)

            def mark_ids(t):
                dve.wait_ge(cd_summed, t + 1)
                if isinstance(t, int) and t > TILES:
                    dve.wait_ge(x_transposed, t + 2)
                else:
                    dve.wait_ge(xT_copied, t + 2)
                nc.vector.tensor_tensor(one_hot[:, 0:CAT_CHUNKS, :], p_ids[:, 0:P].unsqueeze(1).broadcast_to([P, CAT_CHUNKS, P]),
                                        row_numbers[:, :].unsqueeze(2).broadcast_to([P, CAT_CHUNKS, P]), ALU.is_equal)
                nc.vector.tensor_tensor(one_hot[:, CAT_CHUNKS, :], p_ids[:, P:2 * P], row_numbers[:, 0:1].broadcast_to([P, P]),
                                        ALU.is_equal).then_inc(one_hot_ready, 1)

            dve.wait_ge(mlp_loaded, MLP_LOADS)
            dve.wait_ge(users_landed, 16 * TILES)
            dve.sem_inc(dve_passed, 1)
            columns_at = [dve.alloc_register(f"dve_columns_{name}") for name in ("before", "now", "next", "most")]
            dve.reg_mov(columns_at[0], 0)
            dve.reg_mov(columns_at[1], columns_of(dve, 1))
            dve.reg_mov(columns_at[2], columns_of(dve, 2))
            dve.reg_mov(columns_at[3], dve.value_load(needed_most[0:1, 0:1], min_val=0, max_val=HISTORY))
            with dve.Fori(0, TILES) as t:
                columns_before, columns, columns_next, columns_most = (
                    dve.snap(register, min_val=0, max_val=HISTORY) for register in columns_at)
                before = dve.snap(base, min_val=1, max_val=(TILES - 1) * BLOCKS + 1)
                sorted_before = dve.snap(before + blocks_of(columns))
                pooled_before = dve.snap(pooled_base, min_val=1, max_val=TILES * BLOCKS + 1)
                steps_before = dve.snap(t * TILE_STEPS)
                picks = dve.snap(t * TILE_PICKS + 2)
                dve.wait_ge(sort_step, sorted_before * 4)
                dve.wait_ge(pick_step, picks)
                load_keys().then_inc(tile_step, 1)
                nc.vector.tensor_copy(scores[:, bass.ds((t & 1) * COLS, COLS)],
                                      last_score[:, bass.ds(t, 1)].broadcast_to([P, COLS])).then_inc(scores_reset, 1)
                dve.wait_ge(tile_step, steps_before + 1)
                dve.sem_inc(dve_passed, 1)
                for v in range(HEAD - 1):
                    def sort_next():
                        if v < 2:
                            sort_block(t + 1, v, sorted_before + v)
                        if v == 0:
                            pick_features(t, picks)
                        if v == 1:
                            mark_ids(t)
                        if v == 2:
                            with dve.If(t < TILES - 1):
                                sort_block(t + 1, v, sorted_before + v)
                                dve.wait_ge(pick_step, picks + 2)
                                pick_keys(t + 2).then_inc(pick_step, 1)
                            with dve.Else():
                                dve.sem_inc(pick_step, 1)

                    def pool_last():
                        if v < 2:
                            index_head_block(v, sorted_before + v)
                        if v == 0:
                            dve.wait_ge(scored[1], before + 1)
                            softmax(t, steps_before)
                        with dve.If(columns_before > v * BLOCK):
                            pool_block(t + 1, v, pooled_before + v)
                        if v == 2:
                            with dve.If(t < TILES - 1):
                                index_head_block(v, sorted_before + v)
                                dve.wait_ge(pick_step, picks + 3)
                                sum_keys(keys_next[:, :]).then_inc(pick_step, 1)
                            with dve.Else():
                                dve.sem_inc(pick_step, 1)

                    dve_unit(t, before + v, 0, v & 1, sort_next)
                    dve_unit(t, before + v, 1, v & 1, pool_last)
                    if v == 1:
                        columns_later = columns_of(dve, t + 3)
                        columns_most_later = dve.value_load(needed_most[0:1, bass.ds(t + 1, 1)], min_val=0, max_val=HISTORY)
                with dve.If(columns_most > LEAST):
                    v = HEAD - 1
                    with dve.If(columns > LEAST):
                        def sort_next():
                            with dve.If(columns_next > LEAST):
                                sort_block(t + 1, v, sorted_before + v)

                        def pool_last():
                            with dve.If(columns_next > LEAST):
                                index_head_block(v, sorted_before + v)
                            with dve.If(columns_before > LEAST):
                                pool_block(t + 1, v, pooled_before + v)

                        dve_unit(t, before + v, 0, v & 1, sort_next)
                        dve_unit(t, before + v, 1, v & 1, pool_last)
                    with dve.Else():
                        pool_block(t + 1, v, pooled_before + v)
                    with dve.If(columns_most > REST_START):
                        with dve.Fori(0, REST_GROUPS) as group:
                            with dve.If(columns_most > group * (REST_GROUP * BLOCK) + REST_START):
                                with dve.Fori(0, REST_GROUP) as n:
                                    start = dve.snap((group * REST_GROUP + n) * BLOCK + REST_START)
                                    with dve.If(columns > start):
                                        v = block_at(dve, group, n)
                                        dve.reg_add(rest_count, rest_count, 1)
                                        dve.wait_ge(block_sorted, sorted_before)
                                        nc.vector.tensor_copy(
                                            index_rest[:, :], index_rest_sorted[:, bass.ds(t & 1, 1), bass.ds((v - HEAD) * BLOCK, BLOCK)]
                                            .rearrange("p a c -> p (a c)")).then_inc(rest_index_ready, 1)
                                        dve.wait_ge(rest_index_ready, rest_count)
                                        dve.sem_inc(dve_passed, 1)

                                        def sort_next():
                                            with dve.If(columns_next > start):
                                                sort_block(t + 1, v, sorted_before + v)
                                                index_rest_block(t + 1, v)

                                        def pool_last():
                                            with dve.If(columns_before > start):
                                                pool_block(t + 1, v, pooled_before + v)

                                        dve_unit(t, before + v, 0, 0, sort_next)
                                        dve_unit(t, before + v, 1, 0, pool_last)
                                    with dve.Else():
                                        with dve.If(columns_before > start):
                                            v = block_at(dve, group, n)
                                            pool_block(t + 1, v, pooled_before + v)
                                        dve.sem_inc(dve_passed, 1)
                finish_pooling(t + 1)
                dve.wait_ge(history_pooled, t + 2)
                dve.sem_inc(dve_passed, 1)
                dve.reg_add(base, base, dve.snap(blocks_of(columns)))
                dve.reg_add(pooled_base, pooled_base, dve.snap(blocks_of(columns_before)))
                for register, value in zip(columns_at, (columns, columns_next, columns_later, columns_most_later)):
                    dve.reg_mov(register, value)

            columns = dve.snap(columns_at[0], min_val=0, max_val=HISTORY)
            pick_features(TILES, TILES * TILE_PICKS + 2)
            blocks_done = dve.snap(base, min_val=1, max_val=TILES * BLOCKS + 1)
            pooled_before = dve.snap(pooled_base, min_val=1, max_val=TILES * BLOCKS + 1)
            dve.wait_ge(scored[0], blocks_done)
            dve.wait_ge(scored[1], blocks_done + 1)
            softmax(TILES, TILES * TILE_STEPS - 1, lambda: mark_ids(TILES))
            dve.sem_inc(weights_ready, 1)
            pool_block(TILES - 1, 0, pooled_before)
            dve.wait_ge(x_transposed, TILES + 2)
            dve.wait_ge(products_ready, 1)
            sum_features(last_products, TILES + 1)
            dve.wait_ge(weighted_ready, 1)
            nc.vector.tensor_reduce(part[:, :], weighted_two.rearrange("p c d -> p d c"), op=ALU.add, axis=AX.X).then_inc(pool_step, 1)
            dve.wait_ge(pool_step, pooled_before * 3 + 4)
            nc.vector.tensor_tensor(pooled[:, :], pooled[:, :], part[:, :], ALU.add).then_inc(pool_step, 5)
            dve.wait_ge(pool_step, pooled_before * 3 + 9)
            dve.sem_inc(dve_passed, 1)
            mark_ids(TILES + 1)
            with dve.If(columns > LEAST):
                pool_block(TILES - 1, HEAD - 1, pooled_before + (HEAD - 1))
                with dve.If(columns > REST_START):
                    with dve.Fori(0, REST_GROUPS) as group:
                        with dve.Fori(0, REST_GROUP) as n:
                            with dve.If(columns > (group * REST_GROUP + n) * BLOCK + REST_START):
                                v = block_at(dve, group, n)
                                pool_block(TILES - 1, v, pooled_before + v)
            nc.vector.tensor_scalar(x_now[:, X_POOL:X_DIM], pooled[:, :], inv_sum[:, :], None, ALU.mult).then_inc(history_pooled, 1)

            dve.wait_ge(exp_z, 1)
            nc.vector.tensor_scalar(z, z, 1.0, None, ALU.add).then_inc(exp_z, 1)
            dve.wait_ge(exp_z, 2)
            nc.vector.reciprocal(z, z).then_inc(sigmoid_step, 1)
            dve.wait_ge(sigmoid_step, 2)
            nc.vector.tensor_tensor(beats[:, :, :], z.unsqueeze(1).broadcast_to(by_row),
                                    tile_rows.rearrange("p t r -> p r t"), ALU.mult).then_inc(unsort_step, 1)
            dve.wait_ge(unsort_step, 1)
            nc.vector.tensor_reduce(scores_out[:, :], beats[:, :, :], op=ALU.add, axis=AX.X).then_inc(unsort_step, 1)


_INS = ['r_user_dense', 'r_user_id', 'r_item_id', 'r_item_category', 'r_item_dur_bkt', 'r_item_dense', 'r_history_seq',
        'L0_rec_user_W', 'L0_rec_item_W', 'L0_rec_cat_W', 'L0_rec_dur_W', 'L0_rec_hist_W',
        'L0_rec_aW0', 'L0_rec_ab0', 'L0_rec_aW1', 'L0_rec_ab1', 'L0_rec_aW2', 'L0_rec_ab2',
        'L0_rec_mW0', 'L0_rec_mb0', 'L0_rec_mW1', 'L0_rec_mb1', 'L0_rec_mW2', 'L0_rec_mb2']


def kernel(**inputs):
    import numpy as np
    import concourse.bacc as bacc
    from concourse import mybir as _mybir
    from concourse.bass_utils import run_bass_kernel_spmd

    nc = bacc.Bacc("TRN2", target_bir_lowering=False, num_devices=1)
    arrays, args = {}, []
    for name in _INS:
        a = np.ascontiguousarray(inputs[name])
        arrays[f"in_{name}"] = a
        args.append(nc.dram_tensor(f"in_{name}", a.shape, _mybir.dt.from_np(a.dtype), kind="ExternalInput").ap())
    batch = inputs['r_history_seq'].shape[0]
    out = nc.dram_tensor("out_0", [batch], _mybir.dt.float32, kind="ExternalOutput").ap()
    build_recommender(nc, *args, out)
    r = run_bass_kernel_spmd(nc, [arrays], core_ids=[0])
    return r.results[0]["out_0"]
```
